# Optimizing a Trainium2 kernel written in Bass

```python
import numpy as np
import jax
import jax.numpy as jnp

def _softmax(x, axis=-1):
    return jax.nn.softmax(x, axis=axis)

def _gelu(x):
    return jax.nn.gelu(x, approximate=True)

def _silu(x):
    return jax.nn.silu(x)

def _sigmoid(x):
    return jax.nn.sigmoid(x)

def _layernorm(x, axis=-1, eps=1e-05):
    m = jnp.mean(x, axis=axis, keepdims=True)
    v = jnp.var(x, axis=axis, keepdims=True)
    return (x - m) / jnp.sqrt(v + eps)

def _scatter_add(tgt, idx, src, axis=0):
    return tgt.at[idx].add(src)

def _segment_sum(src, seg, n):
    return jax.ops.segment_sum(src, seg, n)
kernel_name = 'mk_decoder_preln_d2_seqx_r8_58d4a9'

def setup_inputs(seed: int=0):
    np.random.seed(seed)
    _w = jnp.asarray

    def _rec_inputs():
        import jax
        import jax.numpy as jnp
        _rk = jax.random.key(seed)
        x = 7.22e-05 + 1 * jax.random.normal(jax.random.fold_in(_rk, 1), (4, 512, 128), jnp.float32)
        _lenS = 512 - jax.random.randint(jax.random.fold_in(_rk, 7), (4,), 0, max(1, 512 // 4) + 1, jnp.int32)
        _lenS2 = 32 - jax.random.randint(jax.random.fold_in(_rk, 8), (4,), 0, max(1, 32 // 4) + 1, jnp.int32)
        _ctx_1024P = jax.random.normal(jax.random.fold_in(_rk, 11), (4, 16, 128), jnp.float32)
        _ctx_1024c = jax.random.dirichlet(jax.random.fold_in(_rk, 511), 0.3 * jnp.ones((16,), jnp.float32), (4, 32))
        _ctx_1024t = jnp.einsum('bsk,bkd->bsd', _ctx_1024c, _ctx_1024P)
        _ctx_1024t = _ctx_1024t * jax.lax.rsqrt(jnp.mean(jnp.square(_ctx_1024t)) + 1e-12) * 0.953939
        ctx_1024 = 4.13588e-05 + 0.999923 * (_ctx_1024t + 0.3 * jax.random.normal(jax.random.fold_in(_rk, 611), (4, 32, 128), jnp.float32))
        fside_BxSxS2_0 = jax.random.uniform(jax.random.fold_in(_rk, 13), (4, 512, 32), jnp.float32, 0.0, 1)
        _validS = jnp.arange(512)[None, :] < _lenS[:, None]
        _validS2 = jnp.arange(32)[None, :] < _lenS2[:, None]
        _causal = jnp.tril(jnp.ones((512, 512), dtype=bool))
        mask_Bx1xS2_ik0 = jnp.where(jnp.broadcast_to(_validS2[:, None, :], (4, 1, 32)), 0, 1).astype(jnp.int32)
        mask_BxSxS2_ik1 = jnp.where(jnp.broadcast_to(_validS2[:, None, :], (4, 512, 32)), 1, 0).astype(jnp.int32)
        return (x, ctx_1024, fside_BxSxS2_0, mask_Bx1xS2_ik0, mask_BxSxS2_ik1)
    x, ctx_1024, fside_BxSxS2_0, mask_Bx1xS2_ik0, mask_BxSxS2_ik1 = _rec_inputs()

    def _L0_attn_setup():
        import jax, jax.numpy as jnp
        import numpy as np
        B, S, E, H = (2, 256, 128, 16)
        HD = E // H
        LAMBDA_INIT = 0.8
        EPS = 1e-06
        key = jax.random.key(seed)
        ks = jax.random.split(key, 8)
        return {'x': jax.random.normal(ks[0], (B, S, E), dtype=jnp.float32), 'w_qkv': jax.random.normal(ks[1], (E, 3 * E), dtype=jnp.float32) * E ** (-0.5), 'wo': jax.random.normal(ks[2], (E, E), dtype=jnp.float32) * E ** (-0.5), 'lambda_q1': jax.random.normal(ks[3], (HD,), dtype=jnp.float32) * 0.1, 'lambda_q2': jax.random.normal(ks[4], (HD,), dtype=jnp.float32) * 0.1, 'lambda_k1': jax.random.normal(ks[5], (HD,), dtype=jnp.float32) * 0.1, 'lambda_k2': jax.random.normal(ks[6], (HD,), dtype=jnp.float32) * 0.1, 'norm_w': jnp.ones((H, HD), dtype=jnp.float32)}
    _L0_attn_all = _L0_attn_setup()
    _L0_attn_in = {k: v for k, v in _L0_attn_all.items() if k in ('w_qkv', 'wo', 'lambda_q1', 'lambda_q2', 'lambda_k1', 'lambda_k2', 'norm_w')}
    del _L0_attn_all

    def _L0_xattn_setup():
        import jax, jax.numpy as jnp
        import numpy as np
        D_MODEL = 128
        NEG_BIG = -1000000000.0
        key = jax.random.key(seed)
        kq, kk, kv, km = jax.random.split(key, 4)
        B, S, D = (4, 256, D_MODEL)
        q = jax.random.normal(kq, (B, S, D), dtype=jnp.float32)
        k = jax.random.normal(kk, (B, S, D), dtype=jnp.float32)
        v = jax.random.normal(kv, (B, S, D), dtype=jnp.float32)
        mask = jax.random.randint(km, (B, 1, S), 0, 2, dtype=jnp.int32)
        return {'q': q, 'k': k, 'v': v, 'mask': mask}
    _L0_xattn_all = _L0_xattn_setup()
    _L0_xattn_in = {k: v for k, v in _L0_xattn_all.items() if k in ()}
    del _L0_xattn_all

    def _L0_ffn_setup():
        import jax, jax.numpy as jnp
        import numpy as np
        EPS = 1e-09
        key = jax.random.key(seed)
        k1, k2, k3, k4 = jax.random.split(key, 4)
        B, T, H, D, E = (2, 256, 128, 128, 8)
        x = jax.random.normal(k1, (B, T, H), dtype=jnp.float32)
        gate_w = jax.random.normal(k2, (E, H), dtype=jnp.float32) * 0.02
        gate_up_proj = jax.random.normal(k3, (E, H, 2 * D), dtype=jnp.float32) * 0.02
        down_proj = jax.random.normal(k4, (E, D, H), dtype=jnp.float32) * 0.02
        return {'x': x, 'gate_w': gate_w, 'gate_up_proj': gate_up_proj, 'down_proj': down_proj}
    _L0_ffn_all = _L0_ffn_setup()
    _L0_ffn_in = {k: v for k, v in _L0_ffn_all.items() if k in ('gate_w', 'gate_up_proj', 'down_proj')}
    del _L0_ffn_all

    def _L1_attn_setup():
        import jax, jax.numpy as jnp
        import numpy as np
        B, T, D = (1, 512, 128)
        HQ, HKV, HD = (16, 4, 64)
        G = HQ // HKV
        NEG = jnp.float32(-1e+30)
        key = jax.random.key(seed)
        ks = jax.random.split(key, 5)
        s = D ** (-0.5)
        return {'x': jax.random.normal(ks[0], (B, T, D), jnp.float32), 'Wq': jax.random.normal(ks[1], (D, HQ * HD), jnp.float32) * s, 'Wk': jax.random.normal(ks[2], (D, HKV * HD), jnp.float32) * s, 'Wv': jax.random.normal(ks[3], (D, HKV * HD), jnp.float32) * s, 'Wo': jax.random.normal(ks[4], (HQ * HD, D), jnp.float32) * s}
    _L1_attn_all = _L1_attn_setup()
    _L1_attn_in = {k: v for k, v in _L1_attn_all.items() if k in ('Wq', 'Wk', 'Wv', 'Wo')}
    del _L1_attn_all

    def _L1_xattn_setup():
        import jax, jax.numpy as jnp
        import numpy as np
        NUM_HEADS = 16
        HIDDEN = 128
        B, S = (2, 256)

        def _split_heads(x, H):
            b, s, d = x.shape
            return x.reshape(b, s, H, d // H).transpose(0, 2, 1, 3)
        key = jax.random.key(seed)
        ks = jax.random.split(key, 14)
        D = HIDDEN
        scale = 1.0 / np.sqrt(D)
        inp = {'query': jax.random.normal(ks[0], (B, S, D), jnp.float32), 'key_in': jax.random.normal(ks[1], (B, S, D), jnp.float32), 'value': jax.random.normal(ks[2], (B, S, D), jnp.float32), 'group_prob': jax.random.uniform(ks[3], (B, S, S), jnp.float32), 'mask': jax.random.randint(ks[4], (B, S, S), 0, 2, jnp.int32), 'wq_k': jax.random.normal(ks[5], (D, D), jnp.float32) * scale, 'wq_b': jnp.zeros((D,), jnp.float32), 'wk_k': jax.random.normal(ks[6], (D, D), jnp.float32) * scale, 'wk_b': jnp.zeros((D,), jnp.float32), 'wv_k': jax.random.normal(ks[7], (D, D), jnp.float32) * scale, 'wv_b': jnp.zeros((D,), jnp.float32), 'wo_k': jax.random.normal(ks[8], (D, D), jnp.float32) * scale, 'wo_b': jnp.zeros((D,), jnp.float32)}
        return inp
    _L1_xattn_all = _L1_xattn_setup()
    _L1_xattn_in = {k: v for k, v in _L1_xattn_all.items() if k in ('wq_k', 'wq_b', 'wk_k', 'wk_b', 'wv_k', 'wv_b', 'wo_k', 'wo_b')}
    del _L1_xattn_all

    def _L1_ffn_setup():
        import jax, jax.numpy as jnp
        import numpy as np
        NUM_EXPERTS = 8
        IN_FEATURES = 128
        HIDDEN_FEATURES = 512
        GATE_DIM = 16
        EPS = 0.0001
        key = jax.random.key(seed)
        ks = jax.random.split(key, 7)
        hidden_states = jax.random.normal(ks[0], (1, 256, IN_FEATURES), dtype=jnp.float32)
        wg_red = jax.random.normal(ks[1], (GATE_DIM, IN_FEATURES), dtype=jnp.float32) * 0.02
        wg = jax.random.normal(ks[2], (NUM_EXPERTS, GATE_DIM), dtype=jnp.float32)
        w1 = jax.random.uniform(ks[3], (NUM_EXPERTS, IN_FEATURES, HIDDEN_FEATURES), dtype=jnp.float32)
        b1 = jax.random.uniform(ks[4], (NUM_EXPERTS, HIDDEN_FEATURES), dtype=jnp.float32)
        w2 = jax.random.uniform(ks[5], (NUM_EXPERTS, HIDDEN_FEATURES, IN_FEATURES), dtype=jnp.float32)
        b2 = jax.random.uniform(ks[6], (NUM_EXPERTS, IN_FEATURES), dtype=jnp.float32)
        return {'hidden_states': hidden_states, 'wg_red': wg_red, 'wg': wg, 'w1': w1, 'b1': b1, 'w2': w2, 'b2': b2}
    _L1_ffn_all = _L1_ffn_setup()
    _L1_ffn_in = {k: v for k, v in _L1_ffn_all.items() if k in ('wg_red', 'wg', 'w1', 'b1', 'w2', 'b2')}
    del _L1_ffn_all
    return {'x': x, 'ctx_1024': ctx_1024, 'fside_BxSxS2_0': fside_BxSxS2_0, 'mask_Bx1xS2_ik0': mask_Bx1xS2_ik0, 'mask_BxSxS2_ik1': mask_BxSxS2_ik1, 'L0_attn_w_qkv': _L0_attn_in['w_qkv'], 'L0_attn_wo': _L0_attn_in['wo'], 'L0_attn_lambda_q1': _L0_attn_in['lambda_q1'], 'L0_attn_lambda_q2': _L0_attn_in['lambda_q2'], 'L0_attn_lambda_k1': _L0_attn_in['lambda_k1'], 'L0_attn_lambda_k2': _L0_attn_in['lambda_k2'], 'L0_attn_norm_w': _L0_attn_in['norm_w'], 'L0_ffn_gate_w': _L0_ffn_in['gate_w'], 'L0_ffn_gate_up_proj': _L0_ffn_in['gate_up_proj'], 'L0_ffn_down_proj': _L0_ffn_in['down_proj'], 'L1_attn_Wq': _L1_attn_in['Wq'], 'L1_attn_Wk': _L1_attn_in['Wk'], 'L1_attn_Wv': _L1_attn_in['Wv'], 'L1_attn_Wo': _L1_attn_in['Wo'], 'L1_xattn_wq_k': _L1_xattn_in['wq_k'], 'L1_xattn_wq_b': _L1_xattn_in['wq_b'], 'L1_xattn_wk_k': _L1_xattn_in['wk_k'], 'L1_xattn_wk_b': _L1_xattn_in['wk_b'], 'L1_xattn_wv_k': _L1_xattn_in['wv_k'], 'L1_xattn_wv_b': _L1_xattn_in['wv_b'], 'L1_xattn_wo_k': _L1_xattn_in['wo_k'], 'L1_xattn_wo_b': _L1_xattn_in['wo_b'], 'L1_ffn_wg_red': _L1_ffn_in['wg_red'], 'L1_ffn_wg': _L1_ffn_in['wg'], 'L1_ffn_w1': _L1_ffn_in['w1'], 'L1_ffn_b1': _L1_ffn_in['b1'], 'L1_ffn_w2': _L1_ffn_in['w2'], 'L1_ffn_b2': _L1_ffn_in['b2']}

def reference(x, ctx_1024, fside_BxSxS2_0, mask_Bx1xS2_ik0, mask_BxSxS2_ik1, L0_attn_w_qkv, L0_attn_wo, L0_attn_lambda_q1, L0_attn_lambda_q2, L0_attn_lambda_k1, L0_attn_lambda_k2, L0_attn_norm_w, L0_ffn_gate_w, L0_ffn_gate_up_proj, L0_ffn_down_proj, L1_attn_Wq, L1_attn_Wk, L1_attn_Wv, L1_attn_Wo, L1_xattn_wq_k, L1_xattn_wq_b, L1_xattn_wk_k, L1_xattn_wk_b, L1_xattn_wv_k, L1_xattn_wv_b, L1_xattn_wo_k, L1_xattn_wo_b, L1_ffn_wg_red, L1_ffn_wg, L1_ffn_w1, L1_ffn_b1, L1_ffn_w2, L1_ffn_b2):
    import jax
    import jax.numpy as jnp

    def _L0_attn_ref(x, w_qkv, wo, lambda_q1, lambda_q2, lambda_k1, lambda_k2, norm_w):
        import jax, jax.numpy as jnp
        import numpy as np
        B, S, E, H = (2, 256, 128, 16)
        HD = E // H
        LAMBDA_INIT = 0.8
        EPS = 1e-06
        b, s, e = x.shape
        qkv = x @ w_qkv
        q, k, v = jnp.split(qkv, 3, axis=-1)

        def to_heads(t):
            return t.reshape(b, s, H, HD).transpose(0, 2, 1, 3)
        q, k, v = (to_heads(q), to_heads(k), to_heads(v))
        q1, q2 = jnp.split(q, 2, axis=-1)
        k1, k2 = jnp.split(k, 2, axis=-1)
        scale = 1.0 / jnp.sqrt(jnp.asarray(HD, dtype=x.dtype))
        a1 = jax.nn.softmax(jnp.einsum('bhsd,bhtd->bhst', q1, k1) * scale, axis=-1)
        a2 = jax.nn.softmax(jnp.einsum('bhsd,bhtd->bhst', q2, k2) * scale, axis=-1)
        lam = jnp.exp(jnp.dot(lambda_q1, lambda_k1)) - jnp.exp(jnp.dot(lambda_q2, lambda_k2)) + LAMBDA_INIT
        a = a1 - lam * a2
        out = jnp.einsum('bhst,bhtd->bhsd', a, v)
        rms = jnp.sqrt(jnp.mean(out * out, axis=-1, keepdims=True) + EPS)
        out_n = out / rms * norm_w[None, :, None, :] * (1.0 - LAMBDA_INIT)
        out_cat = out_n.reshape(b, H * s, HD)
        out_final = out_cat.transpose(0, 2, 1).reshape(b, s, e)
        return out_final @ wo

    def _L0_xattn_ref(q, k, v, mask):
        import jax, jax.numpy as jnp
        import numpy as np
        D_MODEL = 128
        NEG_BIG = -1000000000.0
        scale = jnp.asarray(D_MODEL, q.dtype) ** (-0.5)
        logits = jnp.einsum('bqd,bkd->bqk', q, k) * scale
        logits = logits + mask.astype(q.dtype) * NEG_BIG
        weights = jax.nn.softmax(logits, axis=-1)
        return jnp.einsum('bqk,bkd->bqd', weights, v)

    def _L0_ffn_ref(x, gate_w, gate_up_proj, down_proj):
        import jax, jax.numpy as jnp
        import numpy as np
        EPS = 1e-09
        B, T, H = x.shape
        E = gate_w.shape[0]
        top_k = 2
        hidden = x.reshape(-1, H)
        router_logits = hidden @ gate_w.T
        routing_weights = jax.nn.softmax(router_logits.astype(jnp.float32), axis=-1)
        topk_weights, topk_indices = jax.lax.top_k(routing_weights, top_k)
        topk_weights = topk_weights / (jnp.sum(topk_weights, axis=-1, keepdims=True) + EPS)
        N = hidden.shape[0]
        routed = jnp.zeros((N, E), dtype=router_logits.dtype)
        rows = jnp.arange(N)[:, None]
        routed = routed.at[rows, topk_indices].set(topk_weights.astype(router_logits.dtype))
        routed = routed / (jnp.sum(routed, axis=-1, keepdims=True) + EPS)
        routed = routed.astype(hidden.dtype)
        gate_up = jnp.einsum('th,ehq->teq', hidden, gate_up_proj)
        gate, up = jnp.split(gate_up, 2, axis=-1)
        expert_outputs = jnp.einsum('teq,eqh->teh', jax.nn.silu(gate) * up, down_proj)
        out = jnp.sum(expert_outputs * routed[:, :, None], axis=1)
        return out.reshape(B, T, H)

    def _L1_attn_ref(x, Wq, Wk, Wv, Wo):
        import jax, jax.numpy as jnp
        import numpy as np
        B, T, D = (1, 512, 128)
        HQ, HKV, HD = (16, 4, 64)
        G = HQ // HKV
        NEG = jnp.float32(-1e+30)
        b, t, _ = x.shape
        q = (x @ Wq).reshape(b, t, HKV, G, HD)
        k = (x @ Wk).reshape(b, t, HKV, HD)
        v = (x @ Wv).reshape(b, t, HKV, HD)
        scores = jnp.einsum('bqhgd,bkhd->bhgqk', q, k) / jnp.sqrt(jnp.float32(HD))
        causal = jnp.tril(jnp.ones((t, t), bool))
        scores = jnp.where(causal, scores, NEG)
        attn = jax.nn.softmax(scores, axis=-1)
        ctx = jnp.einsum('bhgqk,bkhd->bqhgd', attn, v).reshape(b, t, HQ * HD)
        return ctx @ Wo

    def _L1_xattn_ref(query, key_in, value, group_prob, mask, wq_k, wq_b, wk_k, wk_b, wv_k, wv_b, wo_k, wo_b):
        import jax, jax.numpy as jnp
        import numpy as np
        NUM_HEADS = 16
        HIDDEN = 128
        B, S = (2, 256)

        def _split_heads(x, H):
            b, s, d = x.shape
            return x.reshape(b, s, H, d // H).transpose(0, 2, 1, 3)
        H = NUM_HEADS
        dh = query.shape[-1] // H
        q = _split_heads(query @ wq_k + wq_b, H)
        k = _split_heads(key_in @ wk_k + wk_b, H)
        v = _split_heads(value @ wv_k + wv_b, H)
        logits = jnp.einsum('bhqd,bhkd->bhqk', q, k) / jnp.sqrt(jnp.asarray(dh, q.dtype))
        neg = (1.0 - mask.astype(q.dtype)) * -1000000000.0
        logits = logits + neg[:, None, :, :]
        attn = jax.nn.softmax(logits, axis=-1)
        attn = attn * group_prob[:, None, :, :]
        out = jnp.einsum('bhqk,bhkd->bhqd', attn, v)
        out = out.transpose(0, 2, 1, 3).reshape(query.shape[0], -1, H * dh)
        return out @ wo_k + wo_b

    def _L1_ffn_ref(hidden_states, wg_red, wg, w1, b1, w2, b2):
        import jax, jax.numpy as jnp
        import numpy as np
        NUM_EXPERTS = 8
        IN_FEATURES = 128
        HIDDEN_FEATURES = 512
        GATE_DIM = 16
        EPS = 0.0001
        b, t, c = hidden_states.shape
        x = hidden_states.reshape(-1, c)
        xr = x @ wg_red.T
        wg_unit = wg / jnp.maximum(jnp.linalg.norm(wg, axis=1, keepdims=True), EPS)
        logits = xr @ wg_unit.T
        gates = jax.nn.softmax(logits, axis=1)
        indices_s = jnp.argmax(gates, axis=1)
        scores = jnp.max(gates, axis=1)
        E = wg.shape[0]
        out = jnp.zeros_like(x)
        for e in range(E):
            mask = (indices_s == e).astype(x.dtype)[:, None]
            h = jax.nn.gelu(x @ w1[e] + b1[e], approximate=False)
            out = out + mask * (h @ w2[e] + b2[e])
        out = out * scores[:, None]
        return out.reshape(b, t, c)
    x = x + _L0_attn_ref(_layernorm(x, axis=-1), L0_attn_w_qkv, L0_attn_wo, L0_attn_lambda_q1, L0_attn_lambda_q2, L0_attn_lambda_k1, L0_attn_lambda_k2, L0_attn_norm_w)
    x = x + _L0_xattn_ref(_layernorm(x, axis=-1), ctx_1024, ctx_1024, mask_Bx1xS2_ik0)
    x = x + _L0_ffn_ref(_layernorm(x, axis=-1), L0_ffn_gate_w, L0_ffn_gate_up_proj, L0_ffn_down_proj)
    x = x + _L1_attn_ref(_layernorm(x, axis=-1), L1_attn_Wq, L1_attn_Wk, L1_attn_Wv, L1_attn_Wo)
    x = x + _L1_xattn_ref(_layernorm(x, axis=-1), ctx_1024, ctx_1024, fside_BxSxS2_0, mask_BxSxS2_ik1, L1_xattn_wq_k, L1_xattn_wq_b, L1_xattn_wk_k, L1_xattn_wk_b, L1_xattn_wv_k, L1_xattn_wv_b, L1_xattn_wo_k, L1_xattn_wo_b)
    x = x + _L1_ffn_ref(_layernorm(x, axis=-1), L1_ffn_wg_red, L1_ffn_wg, L1_ffn_w1, L1_ffn_b1, L1_ffn_w2, L1_ffn_b2)
    return x

_drawn_inputs = setup_inputs


def setup_inputs(seed=0):
    import zlib

    import numpy as np

    out = dict(_drawn_inputs(seed))
    spreads = {'L0_attn_norm_w': (1.0, 0.6),
     'L1_xattn_wq_b': (0.0, 2.0),
     'L1_xattn_wk_b': (0.0, 2.0),
     'L1_xattn_wv_b': (0.0, 0.424),
     'L1_xattn_wo_b': (0.0, 1.039)}
    factors = {'fside_BxSxS2_0': 7.531,
     'L0_attn_lambda_q1': 8.0,
     'L0_attn_lambda_q2': 22.997,
     'L0_attn_lambda_k1': 8.0,
     'L0_attn_lambda_k2': 7.916,
     'L0_ffn_gate_w': 8.0,
     'L0_ffn_gate_up_proj': 8.0,
     'L0_ffn_down_proj': 8.0,
     'L1_ffn_b1': 8.0,
     'L1_ffn_b2': 200.0}
    for name, (base, spread) in spreads.items():
        noise = np.random.default_rng([zlib.crc32(name.encode()), seed]).standard_normal(out[name].shape)
        drawn = base * np.exp(spread * noise) if base else spread * noise
        out[name] = jnp.asarray(drawn.astype(out[name].dtype))
    for name, factor in factors.items():
        out[name] = (out[name] * factor).astype(out[name].dtype)
    return out
```

```python
from contextlib import ExitStack

import concourse.bass as bass
from concourse import mybir

F32 = mybir.dt.float32
BF16 = mybir.dt.bfloat16
I32 = mybir.dt.int32
ALU = mybir.AluOpType
ACT = mybir.ActivationFunctionType
AX_X = mybir.AxisListType.X

P = 128
B, S, D = 4, 512, 128
SB = S // P
NT = B * SB
KEYS = 32

INPUTS = [
    "x", "ctx_1024", "fside_BxSxS2_0", "mask_Bx1xS2_ik0", "mask_BxSxS2_ik1", "L0_attn_w_qkv", "L0_attn_wo",
    "L0_attn_lambda_q1", "L0_attn_lambda_q2", "L0_attn_lambda_k1", "L0_attn_lambda_k2", "L0_attn_norm_w",
    "L0_ffn_gate_w", "L0_ffn_gate_up_proj", "L0_ffn_down_proj", "L1_attn_Wq", "L1_attn_Wk", "L1_attn_Wv",
    "L1_attn_Wo", "L1_xattn_wq_k", "L1_xattn_wq_b", "L1_xattn_wk_k", "L1_xattn_wk_b", "L1_xattn_wv_k",
    "L1_xattn_wv_b", "L1_xattn_wo_k", "L1_xattn_wo_b", "L1_ffn_wg_red", "L1_ffn_wg", "L1_ffn_w1", "L1_ffn_b1",
    "L1_ffn_w2", "L1_ffn_b2",
]


def wait(eng, sem, value):
    if isinstance(value, int) and value <= 0:
        return
    eng.wait_ge(sem, value)


def spread(ap, axis, n):
    ap = ap.unsqueeze(axis)
    shape = list(ap.shape)
    shape[axis] = n
    return ap.broadcast_to(shape)


class Scope:

    def __init__(self, nc, ctx, prefix):
        self.nc, self.ctx, self.prefix, self.sems = nc, ctx, prefix, []
        ctx.callback(self.clear)

    def clear(self):
        if self.sems:
            self.nc.clear_and_free_semaphores(self.sems)
            self.nc.all_engine_barrier()

    def sb(self, name, shape, dt=F32):
        return self.ctx.enter_context(self.nc.sbuf_tensor(f"{self.prefix}_{name}", shape, dt))

    def ps(self, name, shape, dt=F32):
        return self.ctx.enter_context(self.nc.psum_tensor(f"{self.prefix}_{name}", shape, dt))

    def sem(self, name):
        self.sems.append(self.nc.alloc_semaphore(f"{self.prefix}_{name}"))
        return self.sems[-1]

    def block(self):
        return self.ctx.enter_context(self.nc.Block())


class Chain:

    def __init__(self, eng, sem):
        self.eng, self.sem, self.n = eng, sem, 0

    def __call__(self, ins):
        self.n += 1
        ins.then_inc(self.sem, 1)
        self.eng.wait_ge(self.sem, self.n)



class LayerNorm:

    EPS = 1e-5

    def __init__(self, sc, g, psum):
        self.g, self.psum = g, psum
        self.stats = sc.sb("ln_stats", [P, NT, 6])
        self.mv = sc.sb("ln_mv", [P, NT, 2])
        self.ve = sc.sb("ln_ve", [P, NT])
        self.rstd = sc.sb("ln_rstd", [P, NT])
        self.stat, self.aggr, self.eps = sc.sem("ln_stat"), sc.sem("ln_aggr"), sc.sem("ln_eps")
        self.rstd_s, self.norm = sc.sem("ln_rstd"), sc.sem("ln_norm")
        self.turned, self.xt = sc.sem("ln_turned"), sc.sem("ln_xt")

    def vector_stats(self, dve, x_ready=None):
        for b in range(B):
            if x_ready is not None:
                x_ready(dve, b)
            for n in range(SB * b, SB * b + SB):
                dve.bn_stats(self.stats[:, n, :], self.g.X[:, n, :]).then_inc(self.stat, 1)
            for n in range(SB * b, SB * b + SB):
                dve.wait_ge(self.stat, n + 1)
                dve.bn_aggr(self.mv[:, n, :], self.stats[:, n, :]).then_inc(self.aggr, 1)

    def gpsimd(self, pool):
        for b in range(B):
            t = slice(SB * b, SB * b + SB)
            pool.wait_ge(self.aggr, SB * (b + 1))
            pool.tensor_scalar(self.ve[:, t], self.mv[:, t, 1], self.EPS, None, ALU.add).then_inc(self.eps, 1)
            pool.wait_ge(self.eps, b + 1)
            pool.tensor_tensor(self.rstd[:, t], self.ve[:, t], self.g.mhalf[:, 0:SB], ALU.pow).then_inc(self.rstd_s, 1)

    def vector_norm(self, dve):
        for b in range(B):
            dve.wait_ge(self.rstd_s, b + 1)
            for n in range(SB * b, SB * b + SB):
                dve.tensor_scalar(self.g.XN[:, n, :], self.g.X[:, n, :], self.mv[:, n, 0:1],
                                  self.rstd[:, n:n + 1], ALU.subtract, ALU.mult).then_inc(self.norm, 1)

    def tensor(self, pe):
        for b in range(B):
            pe.wait_ge(self.norm, SB * (b + 1))
            wait(pe, self.xt, b - 1)
            for t in range(SB):
                last = pe.transpose(self.psum[b % 2][:, t * P:(t + 1) * P], self.g.XN[:, SB * b + t, :],
                                    self.g.ident[:, :])
            last.then_inc(self.turned, 1)

    def scalar(self, act):
        for b in range(B):
            act.wait_ge(self.turned, b + 1)
            act.activation(self.g.XT[:, b * S:(b + 1) * S], self.psum[b % 2][:, :], ACT.Copy).then_inc(self.xt, 1)

    def ready(self, eng, b):
        eng.wait_ge(self.xt, b + 1)




class Globals:
    pass



H0 = 16
HD0 = D // H0
HALF = HD0 // 2
QUADS = 8
UNITS = B * QUADS
W0 = 32
SHIFT = 24
Q_SLOTS = {"hi": [(0, 3, 1)], "mid": [(3, 2, 1)], "lo": [(5, 1, 1)]}
K_SLOTS = {"hi": [(0, 2, 3), (5, 1, 1)], "mid": [(1, 2, 3)], "lo": [(2, 1, 1)]}


def stage_project0(nc, g, dram, out):
    with ExitStack() as ctx:
        sc = Scope(nc, ctx, "p0")
        bank = [sc.ps(f"bank{i}", [P, 512]) for i in range(2)]
        ln = LayerNorm(sc, g, [sc.ps(f"ln{i}", [P, 512]) for i in range(2)])
        wqkv = sc.sb("wqkv", [P, 3 * D])
        hi = sc.sb("hi", [P, 2, 2 * D], BF16)
        rest = sc.sb("rest", [P, 2, 2 * D])
        mid = sc.sb("mid", [P, 2, 2 * D], BF16)
        lo = sc.sb("lo", [P, 2, 2 * D], BF16)
        x_in = [sc.sem(f"x_in{b}") for b in range(B)]
        w_in, const, tok0, tok1, qkv, s_hi, s_v, s_rest, s_mid, s_lo = (
            sc.sem(n) for n in ("w_in", "const", "q_padded", "k_padded", "qkv", "hi_done", "v_done", "rest_done", "mid_done",
                                "lo_done"))
        placed = {n: sc.sem("placed_" + n) for n in ("pool", "act", "act_hi", "dve")}
        block = sc.block()

        def placements(n, which, part):
            buf = {"hi": hi, "mid": mid, "lo": lo}[part]
            tok, slots, col = {"q": (g.q_tok, Q_SLOTS, 0), "k": (g.k_tok, K_SLOTS, D)}[which]
            units = slice(QUADS * (n // SB), QUADS * (n // SB) + QUADS)
            dst = tok[:, units, n % SB, :].rearrange("p g (j s d) -> p g j s d", s=W0 // HALF, d=HALF)
            src = buf[:, n % 2, col:col + D].rearrange("p (g j d) -> p g j d", g=QUADS, d=HALF)
            return [(dst[:, :, :, s0:s0 + step * (count - 1) + 1:step, :], spread(src, 3, count))
                    for s0, count, step in slots[part]]

        def single_placements(n, which, part):
            return [(to[:, :, :, i, :], src[:, :, :, i, :])
                    for to, src in placements(n, which, part) for i in range(to.shape[3])]

        @block.sync
        def _(sp):
            for b in range(B):
                sp.dma_start(g.X[:, SB * b:SB * b + SB, :],
                             dram["x"][b].rearrange("(t p) d -> p t d", p=P)).then_inc(x_in[b], 16)
            sp.dma_start(wqkv[:, :], dram["L0_attn_w_qkv"]).then_inc(w_in, 16)
            for name in g.weights:
                dst, src = g.weights[name]
                sp.dma_start(dst, src).then_inc(g.w_in[name], 16)

        @block.gpsimd
        def _(pool):
            pool.memset(g.mhalf[:, :], -0.5).then_inc(const, 1)
            pool.memset(g.ident[:, :], 0.0).then_inc(const, 1)
            pool.wait_ge(const, 2)
            pool.affine_select(out=g.ident[:, :], in_=g.ident[:, :], compare_op=ALU.not_equal, fill=1.0, base=0,
                               pattern=[[-1, P]], channel_multiplier=1).then_inc(const, 1)
            pool.wait_ge(const, 3)
            pool.tensor_copy(g.ident16[:, :], g.ident[:, :]).then_inc(const, 1)
            pool.iota(g.rank[:, :], pattern=[[-1, E]], base=E, channel_multiplier=0,
                      allow_small_or_imprecise_dtypes=True).then_inc(const, 1)
            ln.gpsimd(pool)
            v = g.q_tok[:, :, :, :].rearrange("p i t (j w) -> p (i t j) w", w=W0)
            pool.memset(v[:, :, SHIFT:W0], 0.0).then_inc(tok0, 1)
            for n in range(NT):
                pool.wait_ge(s_hi, n + 1)
                for dst, src in placements(n, "q", "hi"):
                    last = pool.tensor_copy(dst, src)
                last.then_inc(placed["pool"], 1)

        @block.vector
        def _(dve):
            v = g.k_tok[:, :, :, :].rearrange("p i t (j w) -> p (i t j) w", w=W0)
            dve.memset(v[:, :, SHIFT:SHIFT + 3], 1.0).then_inc(tok1, 1)
            dve.memset(v[:, :, SHIFT + 3:W0], 0.0).then_inc(tok1, 1)
            ln.vector_stats(dve, lambda e, b: e.wait_ge(x_in[b], 16))
            ln.vector_norm(dve)
            for n in range(NT):
                k = n % 2
                dve.wait_ge(s_hi, n + 1)
                wait(dve, placed["act"], n - 1)
                wait(dve, placed["dve"], n - 1)
                dve.tensor_tensor(rest[:, k, :], bank[k][:, 0:2 * D], hi[:, k, :], ALU.subtract).then_inc(s_rest, 1)
                dve.wait_ge(s_rest, n + 1)
                dve.tensor_copy(mid[:, k, :], rest[:, k, :]).then_inc(s_mid, 1)
                dve.wait_ge(s_mid, n + 1)
                dve.tensor_tensor(lo[:, k, :], rest[:, k, :], mid[:, k, :], ALU.subtract).then_inc(s_lo, 1)
                for dst, src in placements(n, "k", "mid"):
                    dve.tensor_copy(dst, src)
                dve.wait_ge(s_lo, n + 1)
                for dst, src in placements(n, "q", "lo") + placements(n, "k", "lo"):
                    last = dve.tensor_copy(dst, src)
                last.then_inc(placed["dve"], 1)

        @block.tensor
        def _(pe):
            pe.wait_ge(const, 4)
            ln.tensor(pe)
            pe.wait_ge(w_in, 16)
            for n in range(NT):
                ln.ready(pe, n // SB)
                if n >= 2:
                    pe.wait_ge(s_v, n - 1)
                    pe.wait_ge(s_rest, n - 1)
                pe.matmul(bank[n % 2][:, 0:3 * D], g.XT[:, n * P:(n + 1) * P], wqkv[:, :],
                          start=True, stop=True).then_inc(qkv, 1)

        @block.scalar
        def _(act):
            def place_mid(n):
                act.wait_ge(s_mid, n + 1)
                for dst, src in single_placements(n, "q", "mid"):
                    last = act.activation(dst, src, ACT.Copy)
                last.then_inc(placed["act"], 1)

            ln.scalar(act)
            for n in range(NT):
                k = n % 2
                act.wait_ge(qkv, n + 1)
                act.activation(g.v_tok[:, QUADS * (n // SB):QUADS * (n // SB) + QUADS, n % SB, :],
                               bank[k][:, 2 * D:3 * D].rearrange("p (g w) -> p g w", g=QUADS), ACT.Copy).then_inc(s_v, 1)
                wait(act, placed["pool"], n - 1)
                wait(act, s_rest, n - 1)
                wait(act, placed["act_hi"], n - 1)
                act.activation(hi[:, k, :], bank[k][:, 0:2 * D], ACT.Copy).then_inc(s_hi, 1)
                if n:
                    place_mid(n - 1)
                act.wait_ge(s_hi, n + 1)
                for dst, src in single_placements(n, "k", "hi"):
                    last = act.activation(dst, src, ACT.Copy)
                last.then_inc(placed["act_hi"], 1)
            place_mid(NT - 1)



def stage_attention0(nc, g):
    with ExitStack() as ctx:
        sc = Scope(nc, ctx, "a0")
        rows = [sc.ps(f"rows{i}", [P, 2, S]) for i in range(2)]
        turned = [sc.ps(f"turned{i}", [P, S]) for i in range(2)]
        acc = sc.ps("acc", [P, S])
        tp = sc.ps("tp", [P, 2 * S], BF16)
        tpf = tp[:, :].bitcast(F32)
        qk = [sc.sb(f"qk{i}", [P, 2, S], BF16) for i in range(2)]
        q2 = [sc.sb(f"q2{i}", [P, S], BF16) for i in range(2)]
        k_rows = [sc.sb(f"k_rows{i}", [P, 4, S], BF16) for i in range(2)]
        k_turn = [sc.sb(f"k_turn{i}", [P, 4, S], BF16) for i in range(2)]
        probs = sc.sb("probs", [P, 8, S])
        vg = [sc.sb(f"vg{i}", [P, SB, 2, 32]) for i in range(2)]
        nmax = [sc.sb(f"nmax{i}", [P, SB, 4]) for i in range(2)]
        left = sc.sb("left", [P, SB, 4])
        o_sb = sc.sb("o_sb", [P, S])
        o_tok = [sc.sb(f"o_tok{i}", [P, SB * 4, HD0 + 1]) for i in range(2)]
        rsum = [sc.sb(f"rsum{i}", [P, SB * 4]) for i in range(2)]
        o_n = sc.sb("o_n", [P, SB * 4, HD0])
        lamv = sc.sb("lamv", [P, 4, HD0])
        lamp = sc.sb("lamp", [P, 2, HD0])
        lams = sc.sb("lams", [P, 4])
        neglam = sc.sb("neglam", [P, 1])
        (kq_t, kq, kr, kt, row, mx, cut, nm, q2_t, q2_s, t_s, ex, pv, os_, ot, on, rl, vgs, comb, pc, zero0, zero, vzero, lam_in,
         lam) = (sc.sem(n) for n in (
            "kq_turned", "kq_copied", "k_rows_in", "k_turn_in", "row_scores", "row_max", "shift_cut", "shift_placed",
            "q2_turned", "q2_copied", "turned_scores", "exp_done", "pv_done", "acc_copied", "out_turned",
            "out_copied", "recip_done", "v_placed", "combined", "pool_chain", "zeroed_first", "zeroed", "v_zeroed", "lam_in", "lam"))
        block = sc.block()
        N = UNITS

        def run(eng, body):
            for i in range(-1, 3):
                body(i, i % 2, i)
            with eng.Fori(0, (N - 4) // 2) as r:
                for u in range(2):
                    body(2 * r + (3 + u), (3 + u) % 2, 3)
            for i in range(N - 1, N + 2):
                body(i, i % 2, i)

        def has_row(at): return 0 <= at < N
        def has_next(at): return at + 1 < N
        def has_turn(at): return 0 <= at - 1 < N
        def has_out(at): return 0 <= at - 2 < N

        @block.sync
        def _(sp):
            for n, name in enumerate(("L0_attn_lambda_q1", "L0_attn_lambda_k1", "L0_attn_lambda_q2",
                                      "L0_attn_lambda_k2")):
                sp.dma_start(lamv[:, n, :], g.dram[name].partition_broadcast(P)).then_inc(lam_in, 16)
            sp.wait_ge(zero0, 1)

            def body(i, par, at):
                if at == 0:
                    sp.wait_ge(zero, 3)
                if has_row(at):
                    wait(sp, t_s, 16 * (i - 1))
                    for j in range(4):
                        q = slice(32 * j, 32 * j + 32)
                        sp.dma_start(k_turn[par][q, j, :], qk[par][q, 1, :]).then_inc(kt, 16)
                if has_next(at):
                    wait(sp, kq, i + 2)
                    for j in range(4):
                        q = slice(32 * j, 32 * j + 32)
                        sp.dma_start(k_rows[1 - par][q, j, :], qk[1 - par][q, 1, :]).then_inc(kr, 16)

            run(sp, body)

        @block.tensor
        def _(pe):
            def pv_group(i, par, tb):
                pe.wait_ge(ex, 16 * i + 4 * tb + 4)
                if tb == 0:
                    wait(pe, os_, i)
                    pe.wait_ge(vgs, i + 1)
                for j in range(4):
                    last = pe.matmul(acc[32 * j:32 * j + 32, :], vg[par][:, tb, j // 2, :],
                                     probs[:, (tb % 2) * 4 + j, :], start=(tb == 0), stop=(tb == SB - 1))
                last.then_inc(pv, 1)

            def row_pair(i, par, p):
                if p == 0:
                    pe.wait_ge(kr, 64 * (i + 1))
                wait(pe, mx, 8 * i + p - 1)
                sb = p // 2
                for jj in range(2):
                    last = pe.matmul(rows[p % 2][:, jj, :], qk[par][:, 0, sb * P:(sb + 1) * P],
                                     k_rows[par][:, (p % 2) * 2 + jj, :], start=True, stop=True)
                last.then_inc(row, 1)

            def turn_tile(i, par, k):
                if k == 0:
                    pe.wait_ge(q2_s, i + 1)
                    pe.wait_ge(kt, 64 * (i + 1))
                wait(pe, ex, 16 * i + k - 1)
                tb, j = k // 4, k % 4
                pe.matmul(turned[k % 2][:, :], k_turn[par][:, j, tb * P:(tb + 1) * P], q2[par][:, :],
                          start=True, stop=True).then_inc(t_s, 1)

            def body(i, par, at):
                for s in range(8):
                    if has_turn(at):
                        turn_tile(i - 1, 1 - par, 2 * s)
                    if s == 0 and has_next(at):
                        wait(pe, q2_s, i)
                    if s == 6 and has_row(at):
                        pe.wait_ge(nm, i + 1)
                        if has_out(at):
                            pe.wait_ge(on, i - 1)
                        if has_next(at):
                            pe.wait_ge(kq, i + 2)
                    if s < 4 and has_row(at):
                        row_pair(i, par, 4 + s)
                    if s >= 4 and has_next(at):
                        row_pair(i + 1, 1 - par, s - 4)
                    if s == 0 and has_next(at):
                        for half, tok in enumerate((g.q_tok, g.k_tok)):
                            for t in range(SB):
                                last = pe.transpose(tp[:, half * S + t * P:half * S + (t + 1) * P],
                                                    tok[:, i + 1, t, :], g.ident16[:, :])
                        last.then_inc(kq_t, 1)
                    if s == 6 and has_row(at):
                        for t in range(SB):
                            last = pe.transpose(tp[:, t * P:(t + 1) * P], g.q_tok[:, i, t, :], g.ident16[:, :])
                        last.then_inc(q2_t, 1)
                    if has_turn(at):
                        turn_tile(i - 1, 1 - par, 2 * s + 1)
                    if s == 1 and has_out(at):
                        pv_group(i - 2, par, SB - 1)
                    if s in (3, 5, 7) and has_turn(at):
                        pv_group(i - 1, 1 - par, s // 2 - 1)
                    if s == 2 and has_out(at):
                        pe.wait_ge(os_, i - 1)
                        if has_next(at):
                            pe.wait_ge(kq, i + 2)
                        for t in range(SB):
                            last = pe.transpose(tpf[:, t * P:(t + 1) * P], o_sb[:, t * P:(t + 1) * P], g.ident[:, :])
                        last.then_inc(ot, 1)

            run(pe, body)

        @block.vector
        def _(dve):
            dve.memset(k_rows[0][:, :, :], 0.0).then_inc(zero0, 1)
            dve.wait_ge(lam_in, 64)
            dve.tensor_tensor(lamp[:, :, :], lamv[:, 0:4:2, :], lamv[:, 1:4:2, :], ALU.mult).then_inc(lam, 1)
            dve.wait_ge(lam, 1)
            dve.reduce_sum(lams[:, 0:2], lamp[:, :, :], AX_X).then_inc(lam, 1)
            dve.wait_ge(lam, 3)
            dve.tensor_tensor(lams[:, 0:1], lams[:, 3:4], lams[:, 2:3], ALU.subtract).then_inc(lam, 1)
            dve.wait_ge(lam, 4)
            dve.tensor_scalar(neglam[:, :], lams[:, 0:1], -0.8, None, ALU.add).then_inc(lam, 1)

            def pair_max(i, par, p):
                dve.wait_ge(row, 8 * i + p + 1)
                dve.tensor_reduce(nmax[par][:, p // 2, (p % 2) * 2:(p % 2) * 2 + 2], rows[p % 2][:, :, :], AX_X,
                                  ALU.max, negate=True).then_inc(mx, 1)

            def body(i, par, at):
                if has_row(at):
                    pair_max(i, par, 4)
                if has_next(at):
                    dve.wait_ge(kq_t, i + 2)
                    wait(dve, row, 8 * i)
                    wait(dve, kt, 64 * i)
                    dve.tensor_copy(qk[1 - par][:, :, :], tp[:, :].rearrange("p (a s) -> p a s", a=2)).then_inc(kq, 1)
                if has_row(at):
                    for p in range(5, 8):
                        pair_max(i, par, p)
                    base = 3 * i
                    v = g.q_tok[:, i, :, :].rearrange("p t (j w) -> p t j w", w=W0)
                    dve.wait_ge(mx, 8 * i + 8)
                    dve.tensor_copy(v[:, :, :, SHIFT], nmax[par][:, :, :]).then_inc(cut, 1)
                    dve.wait_ge(cut, base + 1)
                    dve.tensor_tensor(left[:, :, :], nmax[par][:, :, :], v[:, :, :, SHIFT],
                                      ALU.subtract).then_inc(cut, 1)
                    dve.wait_ge(cut, base + 2)
                    dve.tensor_copy(v[:, :, :, SHIFT + 1], left[:, :, :]).then_inc(cut, 1)
                    dve.wait_ge(cut, base + 3)
                    dve.tensor_tensor(v[:, :, :, SHIFT + 2], left[:, :, :], v[:, :, :, SHIFT + 1],
                                      ALU.subtract).then_inc(nm, 1)
                if has_next(at):
                    for p in range(4):
                        pair_max(i + 1, 1 - par, p)
                if has_out(at):
                    dve.wait_ge(on, i - 1)
                    wait(dve, comb, i - 3)
                    dve.reciprocal(rsum[par][:, :], o_tok[par][:, :, HD0]).then_inc(rl, 1)

            run(dve, body)

        @block.scalar
        def _(act):
            act.wait_ge(lam, 2)
            act.activation(lams[:, 2:4], lams[:, 0:2], ACT.Exp).then_inc(lam, 1)

            def body(i, par, at):
                for k in range(16):
                    if has_turn(at):
                        act.wait_ge(t_s, 16 * (i - 1) + k + 1)
                        if k % 4 == 0:
                            wait(act, pv, 4 * (i - 1) + k // 4 - 1)
                        act.activation(probs[:, k % 8, :], turned[k % 2][:, :], ACT.Exp,
                                       scale=float(HD0) ** -0.5).then_inc(ex, 1)
                    if k == 3 and has_out(at):
                        act.wait_ge(pv, 4 * (i - 1))
                        wait(act, ot, i - 2)
                        act.activation(o_sb[:, :], acc[:, :], ACT.Copy).then_inc(os_, 1)
                    if k == 7 and has_out(at):
                        act.wait_ge(ot, i - 1)
                        wait(act, comb, i - 3)
                        act.activation(o_tok[par][:, :, :],
                                       tpf.rearrange("p (n w) -> p n w", w=32)[:, :, 0:HD0 + 1],
                                       ACT.Copy).then_inc(on, 1)
                    if k == 14 and has_row(at):
                        act.wait_ge(q2_t, i + 1)
                        act.activation(q2[par][:, :], tp[:, 0:S], ACT.Copy).then_inc(q2_s, 1)

            run(act, body)

        @block.gpsimd
        def _(pool):
            for par in range(2):
                pool.memset(vg[par][:, :, :, :], 0.0).then_inc(vzero, 1)
            pool.wait_ge(vzero, 2)
            for buf in (k_turn[0], k_rows[1], k_turn[1]):
                pool.memset(buf[:, :, :], 0.0).then_inc(zero, 1)
            for par in range(2):
                pool.memset(vg[par][:, :, :, HD0:HD0 + 1], 1.0).then_inc(pc, 1)
            pool.wait_ge(pc, 2)
            pool.wait_ge(lam, 5)

            def body(i, par, at):
                if has_row(at):
                    wait(pool, pv, 4 * (i - 1))
                    v = g.v_tok[:, i, :, :].rearrange("p t (h d) -> p t h d", d=HD0)
                    pool.tensor_copy(vg[par][:, :, :, 0:HD0], v).then_inc(vgs, 1)
                if has_out(at):
                    n = i - 2
                    base = 2 + 2 * n
                    pool.wait_ge(rl, i - 1)
                    half2 = rsum[par][:, :].rearrange("p (n a) -> p n a", a=2)[:, :, 1]
                    pool.tensor_tensor(half2, half2, neglam[:, 0:1].broadcast_to([P, 2 * SB]), ALU.mult).then_inc(pc, 1)
                    pool.wait_ge(pc, base + 1)
                    pool.tensor_tensor(o_n[:, :, :], o_tok[par][:, :, 0:HD0], spread(rsum[par][:, :], 2, HD0),
                                       ALU.mult).then_inc(pc, 1)
                    pool.wait_ge(pc, base + 2)
                    o = o_n[:, :, :].rearrange("p (n a) d -> p n a d", a=2)
                    dst = g.a_unit[:, n, :, :, :].rearrange("p t h d -> p (t h) d")
                    pool.tensor_tensor(dst, o[:, :, 0, :], o[:, :, 1, :], ALU.add).then_inc(comb, 1)

            run(pool, body)


def stage_output0(nc, g):
    with ExitStack() as ctx:
        sc = Scope(nc, ctx, "o0")
        bank = [sc.ps(f"bank{i}", [P, SB, P]) for i in range(2)]
        sq = sc.sb("sq", [P, 2, S])
        ms = sc.sb("ms", [P, B, 64])
        rms = sc.sb("rms", [P, B, 64])
        rinv = sc.sb("rinv", [P, B, 64])
        nw = sc.sb("nw", [P, H0, HD0])
        nwt = sc.sb("nwt", [P, HD0, H0])
        normed = sc.sb("normed", [P, B, S])
        nw_in, s_sq, s_ss, s_ms, s_rt, s_ri, s_n1, s_n2, s_nw, s_mm, s_res, out_s = (sc.sem(n) for n in (
            "nw_in", "sq", "sumsq", "meansq", "root", "recip", "scaled", "normed", "nw", "projected", "residual",
            "out"))
        block = sc.block()

        @block.sync
        def _(sp):
            sp.dma_start(nw[:, :, :], g.dram["L0_attn_norm_w"].partition_broadcast(P)).then_inc(nw_in, 16)

        @block.gpsimd
        def _(pool):
            for b in range(B):
                wait(pool, s_ss, b - 1)
                a = g.a_unit[:, QUADS * b:QUADS * b + QUADS, :, :, :].rearrange("p g t h d -> p (g t h d)")
                pool.tensor_tensor(sq[:, b % 2, :], a, a, ALU.mult).then_inc(s_sq, 1)

        @block.vector
        def _(dve):
            dve.wait_ge(nw_in, 16)
            dve.tensor_scalar(nwt[:, :, :], nw[:, :, :].rearrange("p h d -> p d h"), 1.0 - 0.8, None,
                              ALU.mult).then_inc(s_nw, 1)
            for b in range(B):
                dve.wait_ge(s_sq, b + 1)
                dve.reduce_sum(ms[:, b, :], sq[:, b % 2, :].rearrange("p (r d) -> p r d", d=HD0), AX_X).then_inc(s_ss, 1)
                dve.wait_ge(s_ss, b + 1)
                dve.tensor_scalar(ms[:, b, :], ms[:, b, :], 1.0 / HD0, 1e-6, ALU.mult, ALU.add).then_inc(s_ms, 1)
            dve.wait_ge(s_nw, 1)
            for b in range(B):
                dve.wait_ge(s_rt, b + 1)
                dve.reciprocal(rinv[:, b, :], rms[:, b, :]).then_inc(s_ri, 1)
                dve.wait_ge(s_ri, b + 1)
                a = g.a_unit[:, QUADS * b:QUADS * b + QUADS, :, :, :].rearrange("p g t h d -> p (g t h) d")
                dve.tensor_tensor(a, a, spread(rinv[:, b, :], 2, HD0), ALU.mult).then_inc(s_n1, 1)
                dve.wait_ge(s_n1, b + 1)
                v = normed[:, b, :].rearrange("p (d g h t) -> p d g h t", d=HD0, g=QUADS, h=2)
                for d in range(HD0):
                    last = dve.tensor_tensor(
                        v[:, d, :, :, :].rearrange("p g h t -> p g t h"),
                        g.a_unit[:, QUADS * b:QUADS * b + QUADS, :, :, d],
                        spread(nwt[:, d, :].rearrange("p (g h) -> p g h", h=2), 2, SB), ALU.mult)
                last.then_inc(s_n2, 1)
            for b in range(B):
                dve.wait_ge(s_mm, b + 1)
                x = g.X[:, SB * b:SB * b + SB, :]
                dve.tensor_tensor(x, x, bank[b % 2][:, :, :], ALU.add).then_inc(s_res, 1)

        @block.scalar
        def _(act):
            for b in range(B):
                act.wait_ge(s_ms, b + 1)
                act.activation(rms[:, b, :], ms[:, b, :], ACT.Sqrt).then_inc(s_rt, 1)

        @block.tensor
        def _(pe):
            pe.wait_ge(g.w_in["wo0"], 16)
            for b in range(B):
                pe.wait_ge(s_n2, b + 1)
                wait(pe, s_res, b - 1)
                for t in range(SB):
                    last = pe.matmul(bank[b % 2][:, t, :], normed[:, b, t * P:(t + 1) * P], g.wo0[:, :],
                                     start=True, stop=True)
                last.then_inc(s_mm, 1)



def stage_cross0(nc, g):
    with ExitStack() as ctx:
        sc = Scope(nc, ctx, "c0")
        ln = LayerNorm(sc, g, [sc.ps(f"ln{i}", [P, 512]) for i in range(2)])
        logits = [sc.ps(f"logits{i}", [P, SB, KEYS]) for i in range(2)]
        wt_ps = [sc.ps(f"wt{i}", [P, P]) for i in range(2)]
        o_ps = [sc.ps(f"o{i}", [P, SB, D]) for i in range(2)]
        diag = sc.sb("diag", [P, B, SB, D])
        rows = sc.sb("rows", [KEYS, B, D])
        mask = sc.sb("mask", [P, B, KEYS], I32)
        bias = sc.sb("bias", [P, B, KEYS])
        w = sc.sb("w", [P, B, SB, KEYS])
        nmax = sc.sb("nmax", [P, B, SB])
        rsum = sc.sb("rsum", [P, B, SB])
        wt = sc.sb("wt", [P, B, P])
        zero, ctx_in, mask_in, s_bias, s_ct, s_ctx, s_lg, s_l1, s_nm, s_z, s_e, s_sum, s_r, s_w, s_wt, s_o, s_x = (
            sc.sem(n) for n in ("zero", "ctx_in", "mask_in", "bias", "ctx_turned", "ctx_t", "logits", "biased",
                                "max", "shifted", "exp", "sum", "recip", "w_turned", "w_copied", "out", "residual"))
        block = sc.block()

        @block.sync
        def _(sp):
            sp.dma_start(rows[:, :, :], g.dram["ctx_1024"].rearrange("b k d -> k b d")).then_inc(ctx_in, 16)
            sp.dma_start(mask[:, :, :], g.dram["mask_Bx1xS2_ik0"].rearrange("b o k -> (o b) k").partition_broadcast(P)
                         ).then_inc(mask_in, 16)
            sp.wait_ge(zero, 1)
            for t in range(SB):
                sp.dma_start(diag[KEYS * t:KEYS * t + KEYS, :, t, :],
                             g.dram["ctx_1024"].rearrange("b k d -> k b d")).then_inc(ctx_in, 16)

        @block.gpsimd
        def _(pool):
            pool.memset(diag[:, :, :, :], 0.0).then_inc(zero, 1)
            ln.gpsimd(pool)
            pool.wait_ge(mask_in, 16)
            pool.tensor_scalar(bias[:, :, :], mask[:, :, :], -1e9, None, ALU.mult).then_inc(s_bias, 1)

        @block.vector
        def _(dve):
            ln.vector_stats(dve)
            ln.vector_norm(dve)
            dve.wait_ge(s_bias, 1)
            for b in range(B):
                dve.wait_ge(s_lg, b + 1)
                dve.scalar_tensor_tensor(out=w[:, b], in0=logits[b % 2][:, :, :], scalar=float(D) ** -0.5,
                                         in1=spread(bias[:, b, :], 1, SB), op0=ALU.mult, op1=ALU.add).then_inc(s_l1, 1)
                dve.wait_ge(s_l1, b + 1)
                dve.tensor_reduce(nmax[:, b, :], w[:, b], AX_X, ALU.max, negate=True).then_inc(s_nm, 1)
                dve.wait_ge(s_nm, b + 1)
                dve.tensor_tensor(w[:, b], w[:, b], spread(nmax[:, b, :], 2, KEYS), ALU.add).then_inc(s_z, 1)
            for b in range(B):
                dve.wait_ge(s_e, b + 1)
                dve.reduce_sum(rsum[:, b, :], w[:, b], AX_X).then_inc(s_sum, 1)
            dve.wait_ge(s_sum, B)
            dve.reciprocal(rsum[:, :, :], rsum[:, :, :]).then_inc(s_r, 1)
            dve.wait_ge(s_r, 1)
            for b in range(B):
                dve.wait_ge(s_o, b + 1)
                for t in range(SB):
                    x = g.X[:, SB * b + t, :]
                    last = dve.scalar_tensor_tensor(out=x, in0=o_ps[b % 2][:, t, :], scalar=rsum[:, b, t:t + 1],
                                                    in1=x, op0=ALU.mult, op1=ALU.add)
                last.then_inc(s_x, 1)

        @block.tensor
        def _(pe):
            pe.wait_ge(ctx_in, 16 * 5)
            for b in range(B):
                last = pe.transpose(wt_ps[0][:, KEYS * b:KEYS * b + KEYS], rows[:, b, :], g.ident[0:KEYS, 0:KEYS])
            last.then_inc(s_ct, 1)
            ln.tensor(pe)
            pe.wait_ge(s_ctx, 1)
            for b in range(B):
                ln.ready(pe, b)
                wait(pe, s_l1, b - 1)
                for t in range(SB):
                    n = SB * b + t
                    last = pe.matmul(logits[b % 2][:, t, :], g.XT[:, n * P:(n + 1) * P],
                                     g.ctx_t[:, KEYS * b:KEYS * b + KEYS], start=True, stop=True)
                last.then_inc(s_lg, 1)
            for b in range(B):
                pe.wait_ge(s_e, b + 1)
                wait(pe, s_w, 0)
                wait(pe, s_wt, b - 1)
                pe.transpose(wt_ps[b % 2][:, :], w[:, b].rearrange("p t k -> p (t k)"), g.ident[:, :]).then_inc(s_w, 1)
                pe.wait_ge(s_wt, b + 1)
                wait(pe, s_x, b - 1)
                pe.matmul(o_ps[b % 2][:, :, :].rearrange("p t d -> p (t d)"), wt[:, b, :],
                          diag[:, b].rearrange("p t d -> p (t d)"), start=True, stop=True).then_inc(s_o, 1)

        @block.scalar
        def _(act):
            act.wait_ge(s_ct, 1)
            act.activation(g.ctx_t[:, :], wt_ps[0][:, :], ACT.Copy).then_inc(s_ctx, 1)
            ln.scalar(act)
            for b in range(B):
                act.wait_ge(s_z, b + 1)
                act.activation(w[:, b], w[:, b], ACT.Exp).then_inc(s_e, 1)
            for b in range(B):
                act.wait_ge(s_w, b + 1)
                act.activation(wt[:, b, :], wt_ps[b % 2][:, :], ACT.Copy).then_inc(s_wt, 1)



E = 8


class Router:

    def __init__(self, sc, g):
        self.g = g
        self.p = sc.sb("rt_p", [P, NT, E])
        self.t = sc.sb("rt_t", [P, NT, E])
        self.pick = [sc.sb(f"rt_pick{i}", [P, NT, E]) for i in range(2)]
        self.v = sc.sb("rt_v", [P, NT])
        self.score = sc.sb("rt_score", [P, NT])
        self.route = sc.sb("route", [P, E, NT])
        self.logit_s, self.shifted, self.exp, self.chain, self.done = (
            sc.sem(n) for n in ("rt_logits", "rt_shifted", "rt_exp", "rt_chain", "rt_done"))

    def scalar(self, act):
        act.wait_ge(self.shifted, 1)
        act.activation(self.p[:, :, :], self.p[:, :, :], ACT.Exp).then_inc(self.exp, 1)

    def softmax(self, dve, link, logits):
        dve.wait_ge(self.logit_s, 1)
        link(dve.tensor_reduce(self.v[:, :], logits, AX_X, ALU.max, negate=True))
        dve.tensor_tensor(self.p[:, :, :], logits, spread(self.v[:, :], 2, E), ALU.add).then_inc(self.shifted, 1)
        dve.wait_ge(self.exp, 1)
        link(dve.reduce_sum(self.v[:, :], self.p[:, :, :], AX_X))
        link(dve.reciprocal(self.v[:, :], self.v[:, :]))
        link(dve.tensor_tensor(self.p[:, :, :], self.p[:, :, :], spread(self.v[:, :], 2, E), ALU.mult))

    def first_largest(self, dve, link, p, score, pick):
        link(dve.tensor_reduce(score[:, :], p, AX_X, ALU.max))
        link(dve.tensor_tensor(self.t[:, :, :], p, spread(score[:, :], 2, E), ALU.is_equal))
        link(dve.tensor_tensor(self.t[:, :, :], self.t[:, :, :], spread(self.g.rank[:, :], 1, NT), ALU.mult))
        link(dve.tensor_reduce(self.v[:, :], self.t[:, :, :], AX_X, ALU.max))
        link(dve.tensor_tensor(pick[:, :, :], self.t[:, :, :], spread(self.v[:, :], 2, E), ALU.is_equal))

    def top2(self, dve, logits, eps):
        link = Chain(dve, self.chain)
        self.softmax(dve, link, logits)
        one, two = self.pick
        self.first_largest(dve, link, self.p[:, :, :], self.score, one)
        link(dve.scalar_tensor_tensor(out=two[:, :, :], in0=one[:, :, :], scalar=-2.0, in1=self.p[:, :, :],
                                      op0=ALU.mult, op1=ALU.add))
        self.first_largest(dve, link, two[:, :, :], self.score, two)
        link(dve.tensor_tensor(one[:, :, :], one[:, :, :], two[:, :, :], ALU.add))
        link(dve.tensor_tensor(self.p[:, :, :], self.p[:, :, :], one[:, :, :], ALU.mult))
        for last in (False, True):
            link(dve.reduce_sum(self.v[:, :], self.p[:, :, :], AX_X))
            link(dve.tensor_scalar(self.v[:, :], self.v[:, :], eps, None, ALU.add))
            link(dve.reciprocal(self.v[:, :], self.v[:, :]))
            if not last:
                link(dve.tensor_tensor(self.p[:, :, :], self.p[:, :, :], spread(self.v[:, :], 2, E), ALU.mult))
        dve.tensor_tensor(self.route[:, :, :].rearrange("p e n -> p n e"), self.p[:, :, :],
                          spread(self.v[:, :], 2, E), ALU.mult).then_inc(self.done, 1)

    def top1(self, dve, logits):
        link = Chain(dve, self.chain)
        self.softmax(dve, link, logits)
        self.first_largest(dve, link, self.p[:, :, :], self.score, self.pick[0])
        dve.tensor_tensor(self.route[:, :, :].rearrange("p e n -> p n e"), self.pick[0][:, :, :],
                          spread(self.score[:, :], 2, E), ALU.mult).then_inc(self.done, 1)



def stage_mixture0(nc, g):
    with ExitStack() as ctx:
        sc = Scope(nc, ctx, "m0")
        ln_ps = [sc.ps(f"ln{i}", [P, 512]) for i in range(2)]
        ln = LayerNorm(sc, g, ln_ps)
        rt = Router(sc, g)
        gate = [sc.ps(f"gate{i}", [P, S]) for i in range(2)]
        up = [sc.ps(f"up{i}", [P, S]) for i in range(2)]
        down = [sc.ps(f"down{i}", [P, SB, D]) for i in range(2)]
        gw = sc.sb("gw", [E, D])
        gwt = sc.sb("gwt", [P, E])
        wgu = [sc.sb(f"wgu{i}", [P, 2 * D]) for i in range(2)]
        wdn = [sc.sb(f"wdn{i}", [P, D]) for i in range(2)]
        silu = [sc.sb(f"silu{i}", [P, S]) for i in range(2)]
        hid = [sc.sb(f"hid{i}", [P, S]) for i in range(2)]
        w_in = [sc.sem(f"w_in{i}") for i in range(2)]
        gw_in, gw_t, gw_s, s_gu, s_silu, s_h, s_dn, s_x = (
            sc.sem(n) for n in ("gw_in", "gw_turned", "gw_copied", "gate_up", "silu", "hidden", "down",
                                "residual"))
        block = sc.block()
        T = E * B

        def run(eng, body):
            body(0, True)
            with eng.Fori(1, E // 2) as r:
                body(r, False)

        @block.sync
        def _(sp):
            sp.dma_start(gw[:, :], g.dram["L0_ffn_gate_w"]).then_inc(gw_in, 16)

            def body(r, first):
                for u in range(2):
                    e = 2 * r + u
                    if not first:
                        sp.wait_ge(s_dn, 4 * (e - 1))
                    sp.dma_start(wgu[u][:, :], g.dram["L0_ffn_gate_up_proj"][e]).then_inc(w_in[u], 16)
                    sp.dma_start(wdn[u][:, :], g.dram["L0_ffn_down_proj"][e]).then_inc(w_in[u], 16)

            run(sp, body)

        @block.gpsimd
        def _(pool):
            ln.gpsimd(pool)

        @block.tensor
        def _(pe):
            pe.wait_ge(gw_in, 16)
            pe.transpose(gate[0][:, 0:E], gw[:, :], g.ident[0:E, 0:E]).then_inc(gw_t, 1)
            ln.tensor(pe)
            pe.wait_ge(gw_s, 1)
            ln.ready(pe, B - 1)
            for n in range(NT):
                last = pe.matmul(ln_ps[0][:, n * E:(n + 1) * E], g.XT[:, n * P:(n + 1) * P], gwt[:, :],
                                 start=True, stop=True)
            last.then_inc(rt.logit_s, 1)

            def down_of(t, u):
                pe.wait_ge(s_h, t + 1)
                wait(pe, s_x, t - 1)
                k = u % 2
                for i in range(SB):
                    last = pe.matmul(down[k][:, i, :], hid[k][:, i * P:(i + 1) * P], wdn[(u // B) % 2][:, :],
                                     start=True, stop=True)
                last.then_inc(s_dn, 1)

            def body(r, first):
                for u in range(2 * B):
                    t = 2 * B * r + u
                    if u % B == 0:
                        pe.wait_ge(w_in[u // B], 32 * (r + 1))
                    wait(pe, s_silu, t - 1)
                    wait(pe, s_h, t - 1)
                    k, b = u % 2, u % B
                    for half, dst in ((0, gate[k]), (1, up[k])):
                        last = pe.matmul(dst[:, :], wgu[u // B][:, half * D:(half + 1) * D],
                                         g.XT[:, b * S:(b + 1) * S], start=True, stop=True)
                    last.then_inc(s_gu, 1)
                    if not (first and u == 0):
                        down_of(t - 1, (u - 1) % (2 * B))

            run(pe, body)
            down_of(T - 1, 2 * B - 1)

        @block.scalar
        def _(act):
            act.wait_ge(gw_t, 1)
            act.activation(gwt[:, :], gate[0][:, 0:E], ACT.Copy).then_inc(gw_s, 1)
            ln.scalar(act)
            rt.scalar(act)

            def body(r, first):
                for u in range(2 * B):
                    t = 2 * B * r + u
                    act.wait_ge(s_gu, t + 1)
                    wait(act, s_h, t - 1)
                    act.activation(silu[u % 2][:, :], gate[u % 2][:, :], ACT.Silu).then_inc(s_silu, 1)

            run(act, body)

        @block.vector
        def _(dve):
            ln.vector_stats(dve)
            ln.vector_norm(dve)
            rt.top2(dve, ln_ps[0][:, 0:NT * E].rearrange("p (n e) -> p n e", e=E), 1e-9)
            dve.wait_ge(rt.done, 1)

            def add(t, e, u):
                dve.wait_ge(s_dn, t + 1)
                for i in range(SB):
                    n = SB * (u % B) + i
                    x = g.X[:, n, :]
                    last = dve.scalar_tensor_tensor(out=x, in0=down[u % 2][:, i, :], scalar=rt.route[:, e, n:n + 1],
                                                    in1=x, op0=ALU.mult, op1=ALU.add)
                last.then_inc(s_x, 1)

            def body(r, first):
                for u in range(2 * B):
                    t = 2 * B * r + u
                    dve.wait_ge(s_silu, t + 1)
                    wait(dve, s_dn, t - 1)
                    dve.tensor_tensor(hid[u % 2][:, :], silu[u % 2][:, :], up[u % 2][:, :],
                                      ALU.mult).then_inc(s_h, 1)
                    if not (first and u == 0):
                        add(t - 1, 2 * r + (u - 1) // B, (u - 1) % (2 * B))

            run(dve, body)
            add(T - 1, E - 1, 2 * B - 1)



HQ, HKV, HD1 = 16, 4, 64
GROUP = HQ // HKV
UNITS1 = B * HKV


def stage_attention1(nc, g):
    with ExitStack() as ctx:
        sc = Scope(nc, ctx, "a1")
        score = [sc.ps(f"score{i}", [P, S]) for i in range(SB)]
        turn = [sc.ps(f"turn{i}", [P, S]) for i in range(2)]
        acc = sc.ps("acc", [P, S])
        misc = sc.ps("misc", [P, S])
        ln = LayerNorm(sc, g, turn)
        wv = sc.sb("wv", [P, HKV * HD1])
        wo = sc.sb("wo", [P, HQ // 2, D])
        wq = [sc.sb(f"wq{i}", [P, GROUP * HD1]) for i in range(2)]
        wk = [sc.sb(f"wk{i}", [P, 2, HD1]) for i in range(2)]
        vals = sc.sb("vals", [P, UNITS1, SB, HD1])
        v_s = [sc.sb(f"v_s{i}", [P, SB, HD1]) for i in range(2)]
        k_s = [[sc.sb(f"k_s{i}{j}", [P, S]) for j in range(2)] for i in range(2)]
        q_s = [[sc.sb(f"q_s{i}{j}", [P, S]) for j in range(2)] for i in range(2)]
        prob = [sc.sb(f"prob{i}", [P, SB, S]) for i in range(2)]
        pt = [sc.sb(f"pt{i}", [P, SB, S]) for i in range(4)]
        ct = [sc.sb(f"ct{i}", [P, S]) for i in range(2)]
        nmax = sc.sb("nmax", [P, 2, SB])
        rsum = sc.sb("rsum", [P, 2, SB])
        rinv = sc.sb("rinv", [P, 2, SB])
        causal = sc.sb("causal", [P, P], BF16)
        w_q_in = [sc.sem(f"wq_in{i}") for i in range(2)]
        (wv_in, wo_in, zero, cz, v_mm, v_ev, vcp, pj, pje, s_s, mx, ex, ri, scl, tps, eva, evd, pvs, cte, ys,
         ye) = (sc.sem(n) for n in (
            "wv_in", "wo_in", "zeroed", "causal_ready", "v_projected", "v_copied", "v_placed", "projected", "proj_copied",
            "scores", "max", "exp", "recip", "divided", "turned", "turn_copied_act", "turn_copied_dve", "pv",
            "context_copied", "y", "residual"))
        block = sc.block()
        N = UNITS1

        def run(eng, body):
            body(0, 0, 0)
            with eng.Fori(0, (N - 2) // 2) as r:
                for u in range(2):
                    body(2 * r + (1 + u), (1 + u) % 2, 1)
            body(N - 1, (N - 1) % 2, N - 1)
            body(N, N % 2, N)

        def has_unit(at): return at < N
        def has_next(at): return at + 1 < N
        def has_last(at): return at >= 1

        def batch_of(eng, i):
            return i // HKV

        def head_of(eng, i):
            return i % HKV

        @block.sync
        def _(sp):
            def load(i, par):
                h = head_of(sp, i)
                sp.dma_start(wq[par][:, :], g.dram["L1_attn_Wq"].rearrange("d (h w) -> h d w", h=HKV)[h]).then_inc(
                    w_q_in[par], 16)
                for j in range(2):
                    sp.dma_start(wk[par][:, j, :], g.dram["L1_attn_Wk"].rearrange("d (h w) -> h d w", h=HKV)[h]
                                 ).then_inc(w_q_in[par], 16)

            sp.dma_start(wv[:, :], g.dram["L1_attn_Wv"]).then_inc(wv_in, 16)
            load(0, 0)
            load(1, 1)
            sp.dma_start(wo[:, :, :], g.dram["L1_attn_Wo"].rearrange("(a p) d -> p a d", p=P)).then_inc(wo_in, 16)

            def body(i, par, at):
                if at + 2 < N:
                    sp.wait_ge(pj, 3 * (i + 1))
                    load(i + 2, par)

            body(0, 0, 0)
            with sp.Fori(0, (N - 4) // 2) as r:
                for u in range(2):
                    body(2 * r + (1 + u), (1 + u) % 2, 1)
            body(N - 3, (N - 3) % 2, N - 3)

        @block.gpsimd
        def _(pool):
            pool.memset(causal[:, :], 0.0).then_inc(cz, 1)
            pool.wait_ge(cz, 1)
            pool.affine_select(out=causal[:, :], in_=causal[:, :], compare_op=ALU.is_ge, fill=-1e30, base=0,
                               pattern=[[-1, P]], channel_multiplier=1).then_inc(cz, 1)
            ln.gpsimd(pool)
            pool.wait_ge(v_ev, NT)

            def body(i, par, at):
                if has_unit(at):
                    wait(pool, pvs, 2 * (i - 1))
                    pool.tensor_copy(v_s[par][:, :, :], vals[:, i, :, :]).then_inc(vcp, 1)

            run(pool, body)

        @block.tensor
        def _(pe):
            ln.tensor(pe)
            pe.wait_ge(wv_in, 16)
            for n in range(NT):
                ln.ready(pe, n // SB)
                wait(pe, v_ev, n - 3)
                pe.matmul(score[n % 4][:, 0:HKV * HD1], g.XT[:, n * P:(n + 1) * P], wv[:, :],
                          start=True, stop=True).then_inc(v_mm, 1)
            pe.wait_ge(v_ev, NT)
            pe.wait_ge(cz, 2)
            pe.wait_ge(zero, 4)

            def project(i, par, which):
                b = batch_of(pe, i)
                if which == 0:
                    pe.wait_ge(w_q_in[par], 48 * ((i >> 1) + 1))
                w = (wk[par][:, :, :].rearrange("p a d -> p (a d)") if which == 0 else
                     wq[par][:, (which - 1) * P:which * P])
                x = g.XT[:, b * S:(b + 1) * S] if isinstance(b, int) else g.XT[:, bass.ds(b * S, S)]
                pe.matmul(misc[:, :], w, x, start=True, stop=True).then_inc(pj, 1)

            def scores_of(i, par, m, sb):
                n4 = 16 * i + 4 * m
                width = (sb + 1) * P
                wait(pe, ex, n4 + sb - 3)
                if sb == 0 and m in (0, 2):
                    pe.wait_ge(pje, 4 * i + (3 if m == 0 else 4))
                pe.matmul(score[sb][:, 0:width], q_s[par][m // 2][:, sb * P:(sb + 1) * P],
                          k_s[par][m % 2][:, 0:width], start=True, stop=False)
                pe.matmul(score[sb][:, sb * P:width], g.ident16[:, :], causal[:, :],
                          start=False, stop=True).then_inc(s_s, 1)

            def turn_of(i, par, m, sb):
                n = 4 * i + m
                pe.wait_ge(scl, 16 * i + 4 * m + sb + 1)
                if sb < 2:
                    wait(pe, eva, 2 * n - 1 + sb)
                else:
                    pe.wait_ge(evd, 2 * n + sb - 1)
                for tb in range(sb + 1):
                    last = pe.transpose(turn[sb % 2][:, tb * P:(tb + 1) * P],
                                        prob[m % 2][:, sb, tb * P:(tb + 1) * P], g.ident[:, :])
                last.then_inc(tps, 1)

            def pv_of(i, par, p):
                q = 2 * i + p
                pe.wait_ge(eva, 4 * q + 4)
                pe.wait_ge(evd, 4 * q + 4)
                wait(pe, cte, q)
                pe.wait_ge(vcp, i + 1)
                for tb in range(SB):
                    for j in range(2):
                        last = pe.matmul(acc[j * HD1:(j + 1) * HD1, tb * P:S], v_s[par][:, tb, :],
                                         pt[2 * p + j][:, tb, tb * P:S], start=(tb == 0), stop=(tb == SB - 1))
                last.then_inc(pvs, 1)

            def y_of(i):
                h = head_of(pe, i)
                pe.wait_ge(cte, 2 * (i + 1))
                for sb in range(SB):
                    for p in range(2):
                        w = wo[:, 2 * h + p, :]
                        last = pe.matmul(misc[:, sb * P:(sb + 1) * P], ct[p][:, sb * P:(sb + 1) * P], w,
                                         start=(p == 0), stop=(p == 1))
                last.then_inc(ys, 1)

            project(0, 0, 0)
            pe.wait_ge(pje, 2)
            project(0, 0, 1)
            pe.wait_ge(wo_in, 16)

            def body(i, par, at):
                for m in range(GROUP):
                    for sb in range(SB):
                        if has_unit(at):
                            scores_of(i, par, m, sb)
                        if m >= 1 and has_unit(at):
                            turn_of(i, par, m - 1, sb)
                        if m == 0 and has_last(at):
                            turn_of(i - 1, 1 - par, GROUP - 1, sb)
                        if m == 0 and sb == 1 and has_unit(at):
                            pe.wait_ge(pje, 4 * i + 3)
                            project(i, par, 2)
                        if m == 2 and sb == 1 and has_last(at):
                            if has_unit(at):
                                pe.wait_ge(pje, 4 * (i + 1))
                            y_of(i - 1)
                        if m == 3 and sb == 1 and has_next(at):
                            if has_last(at):
                                pe.wait_ge(ye, i)
                            pe.wait_ge(pje, 4 * (i + 1))
                            project(i + 1, 1 - par, 0)
                        if m == 3 and sb == 3 and has_next(at):
                            pe.wait_ge(pje, 4 * (i + 1) + 2)
                            project(i + 1, 1 - par, 1)
                    if m == 1 and has_last(at):
                        pv_of(i - 1, 1 - par, 1)
                    if m == 3 and has_unit(at):
                        pv_of(i, par, 0)

            run(pe, body)

        @block.scalar
        def _(act):
            ln.scalar(act)
            for n in range(NT):
                act.wait_ge(v_mm, n + 1)
                act.activation(vals[:, HKV * (n // SB):HKV * (n // SB) + HKV, n % SB, :],
                               score[n % 4][:, 0:HKV * HD1].rearrange("p (h d) -> p h d", h=HKV),
                               ACT.Copy).then_inc(v_ev, 1)

            def copy_projection(i, par, which):
                act.wait_ge(pj, 3 * i + which + 1)
                if which == 0:
                    for j in range(2):
                        rows = slice(j * HD1, (j + 1) * HD1)
                        act.activation(k_s[par][j][rows, :], misc[rows, :], ACT.Copy,
                                       scale=float(HD1) ** -0.5).then_inc(pje, 1)
                else:
                    act.activation(q_s[par][which - 1][:, :], misc[:, :], ACT.Copy).then_inc(pje, 1)

            for which in range(2):
                copy_projection(0, 0, which)

            def exp_of(i, m, sb):
                width = (sb + 1) * P
                act.wait_ge(mx, 16 * i + 4 * m + sb + 1)
                wait(act, tps, 16 * i + 4 * m + sb - 7)
                act.activation(prob[m % 2][:, sb, 0:width], score[sb][:, 0:width], ACT.Exp,
                               bias=nmax[:, m % 2, sb:sb + 1], accum_out=rsum[:, m % 2, sb:sb + 1]).then_inc(ex, 1)

            def copy_turn(i, m, sb):
                act.wait_ge(tps, 16 * i + 4 * m + sb + 1)
                if sb == 2:
                    wait(act, pvs, 2 * i + m // 2 - 1)
                act.activation(pt[m][:, 0:sb + 1, sb * P:(sb + 1) * P],
                               turn[sb % 2][:, 0:(sb + 1) * P].rearrange("p (a s) -> p a s", s=P),
                               ACT.Copy).then_inc(eva, 1)

            def copy_context(i, p):
                act.wait_ge(pvs, 2 * i + p + 1)
                wait(act, ys, i)
                act.activation(ct[p][:, :], acc[:, :], ACT.Copy).then_inc(cte, 1)

            def body(i, par, at):
                for m in range(GROUP):
                    for sb in range(SB):
                        if sb >= 2:
                            if m >= 1 and has_unit(at):
                                copy_turn(i, m - 1, sb)
                            if m == 0 and has_last(at):
                                copy_turn(i - 1, GROUP - 1, sb)
                        if has_unit(at):
                            exp_of(i, m, sb)
                        if m == 0 and sb == 1 and has_last(at):
                            copy_context(i - 1, 0)
                        if m == 2 and sb == 0 and has_last(at):
                            copy_context(i - 1, 1)
                        if m == 0 and sb == 2 and has_unit(at):
                            copy_projection(i, par, 2)
                        if m == 3 and sb == 1 and has_next(at):
                            copy_projection(i + 1, 1 - par, 0)
                        if m == 3 and sb == 3 and has_next(at):
                            copy_projection(i + 1, 1 - par, 1)

            run(act, body)

        @block.vector
        def _(dve):
            for i in range(2):
                dve.memset(k_s[i][0][HD1:P, :], 0.0).then_inc(zero, 1)
                dve.memset(k_s[i][1][0:HD1, :], 0.0).then_inc(zero, 1)
            ln.vector_stats(dve)
            ln.vector_norm(dve)

            def max_of(i, m, sb):
                width = (sb + 1) * P
                dve.wait_ge(s_s, 16 * i + 4 * m + sb + 1)
                dve.tensor_reduce(nmax[:, m % 2, sb:sb + 1], score[sb][:, 0:width], AX_X, ALU.max,
                                  negate=True).then_inc(mx, 1)

            def divide(i, m, sb):
                width = (sb + 1) * P
                n = 16 * i + 4 * m + sb
                dve.wait_ge(ex, n + 1)
                dve.reciprocal(rinv[:, m % 2, sb:sb + 1], rsum[:, m % 2, sb:sb + 1]).then_inc(ri, 1)
                dve.wait_ge(ri, n + 1)
                pr = prob[m % 2][:, sb, 0:width]
                dve.tensor_scalar(pr, pr, rinv[:, m % 2, sb:sb + 1], None, ALU.mult).then_inc(scl, 1)

            def copy_turn(i, m, sb):
                dve.wait_ge(tps, 16 * i + 4 * m + sb + 1)
                if sb == 0:
                    wait(dve, pvs, 2 * i + m // 2 - 1)
                dve.tensor_copy(pt[m][:, 0:sb + 1, sb * P:(sb + 1) * P],
                                turn[sb % 2][:, 0:(sb + 1) * P].rearrange("p (a s) -> p a s", s=P)).then_inc(evd, 1)

            def body(i, par, at):
                for m in range(GROUP):
                    def before(sb):
                        if m >= 1 and has_unit(at):
                            copy_turn(i, m - 1, sb)
                        if m == 0 and has_last(at):
                            copy_turn(i - 1, GROUP - 1, sb)

                    if has_unit(at):
                        max_of(i, m, 0)
                        max_of(i, m, 1)
                    before(0)
                    if has_unit(at):
                        divide(i, m, 0)
                        max_of(i, m, 2)
                    before(1)
                    if has_unit(at):
                        divide(i, m, 1)
                        max_of(i, m, 3)
                    if m == 2 and has_last(at):
                        b = batch_of(dve, i - 1)
                        dve.wait_ge(ys, i)
                        x = (g.X[:, SB * b:SB * b + SB, :] if isinstance(b, int) else
                             g.X[:, bass.ds(b * SB, SB), :])
                        dve.tensor_tensor(x, x, misc[:, :].rearrange("p (t d) -> p t d", d=D), ALU.add
                                          ).then_inc(ye, 1)
                    if has_unit(at):
                        divide(i, m, 2)
                        divide(i, m, 3)

            run(dve, body)



H2 = 16
HD2 = D // H2
HK = H2 * KEYS
TURNS = HK // P


def stage_cross1(nc, g):
    with ExitStack() as ctx:
        sc = Scope(nc, ctx, "c1")
        ln_ps = [sc.ps(f"ln{i}", [P, 512]) for i in range(2)]
        ln = LayerNorm(sc, g, ln_ps)
        logits = [sc.ps(f"logits{i}", [P, H2, KEYS]) for i in range(2)]
        turn = [sc.ps(f"turn{i}", [P, TURNS, P]) for i in range(2)]
        o_ps = [sc.ps(f"o{i}", [P, SB, P]) for i in range(2)]
        wq, wk, wv, wo = (sc.sb(n, [P, D]) for n in ("wq", "wk", "wv", "wo"))
        bqk = sc.sb("bqk", [P, 2])
        bv, bo = (sc.sb(n, [P, D]) for n in ("bv", "bo"))
        hmask = sc.sb("hmask", [P, H2])
        mask = sc.sb("mask", [P, NT, KEYS], I32)
        bias = sc.sb("bias", [P, NT, KEYS])
        gp = sc.sb("gp", [P, NT, KEYS])
        ctx4 = sc.sb("ctx4", [P, B, 4, KEYS])
        kt = sc.sb("kt", [P, B * KEYS])
        kd = sc.sb("kd", [P, B, HK])
        vd = sc.sb("vd", [P, B, 640])
        qt = sc.sb("qt", [P, B, S])
        w = [sc.sb(f"w{i}", [P, H2, KEYS]) for i in range(3)]
        wt = [sc.sb(f"wt{i}", [P, TURNS, P]) for i in range(2)]
        nmax = sc.sb("nmax", [P, 3, H2])
        rsum = sc.sb("rsum", [P, 3, H2])
        on = [sc.sb(f"on{i}", [P, D]) for i in range(2)]
        ot = [sc.sb(f"ot{i}", [P, S]) for i in range(2)]
        w_in = [sc.sem(f"w_in{i}") for i in range(4)]
        (b_in, m_in, vz, hm, s_bias, c4, s_kt, s_ktc, s_kd, s_v, s_vd, s_q, s_qc, s_lg, s_l1, s_nm, s_z, s_e, s_sum,
         s_r, s_w, s_wt, s_wtc, s_o, s_on, s_ot, s_otc, s_y, s_x, s_xb) = (sc.sem(n) for n in (
            "biases_in", "mask_in", "v_zeroed", "head_mask", "bias", "ctx4", "k_projected", "k_copied", "k_placed",
            "v_projected", "v_placed", "q_projected", "q_copied", "logits", "biased", "max", "shifted", "exp", "sum",
            "recip", "gated", "w_turned", "w_copied", "out", "out_normed", "out_turned", "out_copied", "y",
            "residual", "bias_added"))
        block = sc.block()

        @block.sync
        def _(sp):
            for i, (dst, name) in enumerate(((wk, "L1_xattn_wk_k"), (wv, "L1_xattn_wv_k"), (wq, "L1_xattn_wq_k"),
                                             (wo, "L1_xattn_wo_k"))):
                sp.dma_start(dst[:, :], g.dram[name]).then_inc(w_in[i], 16)
            sp.dma_start(bqk[:, 0:1], g.dram["L1_xattn_wq_b"].rearrange("(p a) -> p a", a=1)).then_inc(b_in, 16)
            sp.dma_start(bqk[:, 1:2], g.dram["L1_xattn_wk_b"].rearrange("(p a) -> p a", a=1)).then_inc(b_in, 16)
            sp.dma_start(bv[:, :], g.dram["L1_xattn_wv_b"].partition_broadcast(P)).then_inc(b_in, 16)
            sp.dma_start(bo[:, :], g.dram["L1_xattn_wo_b"].partition_broadcast(P)).then_inc(b_in, 16)
            for dst, name in ((mask, "mask_BxSxS2_ik1"), (gp, "fside_BxSxS2_0")):
                sp.dma_start(dst[:, :, :], g.dram[name].rearrange("b (t p) k -> p (b t) k", p=P)).then_inc(m_in, 16)

        @block.gpsimd
        def _(pool):
            ln.gpsimd(pool)
            pool.memset(hmask[:, :], 1.0).then_inc(hm, 1)
            pool.wait_ge(hm, 1)
            pool.affine_select(out=hmask[:, :], in_=hmask[:, :], compare_op=ALU.is_ge, fill=0.0, base=0,
                               pattern=[[-HD2, H2]], channel_multiplier=1).then_inc(hm, 1)
            pool.wait_ge(hm, 2)
            pool.affine_select(out=hmask[:, :], in_=hmask[:, :], compare_op=ALU.is_ge, fill=0.0, base=HD2 - 1,
                               pattern=[[HD2, H2]], channel_multiplier=-1).then_inc(hm, 1)
            pool.memset(vd[:, :, :], 0.0).then_inc(vz, 1)
            pool.wait_ge(m_in, 32)
            pool.tensor_scalar(bias[:, :, :], mask[:, :, :], -1.0, 1e9, ALU.add, ALU.mult).then_inc(s_bias, 1)
            for n in range(NT):
                pool.wait_ge(s_sum, n + 1)
                pool.tensor_tensor(w[n % 3][:, :, :], w[n % 3][:, :, :], spread(gp[:, n, :], 1, H2),
                                   ALU.mult).then_inc(s_w, 1)

        @block.tensor
        def _(pe):
            pe.wait_ge(w_in[0], 16)
            pe.matmul(logits[0][:, 0:4, :].rearrange("p a k -> p (a k)"), wk[:, :], g.ctx_t[:, :], start=True,
                      stop=True).then_inc(s_kt, 1)
            pe.wait_ge(w_in[1], 16)
            pe.wait_ge(c4, 1)
            for b in range(B):
                last = pe.matmul(o_ps[0][:, b, :], ctx4[:, b].rearrange("p a k -> p (a k)"), wv[:, :],
                                 start=True, stop=True)
            last.then_inc(s_v, 1)
            ln.tensor(pe)
            pe.wait_ge(w_in[2], 16)
            for b in range(B):
                ln.ready(pe, b)
                if b < 2:
                    ln.ready(pe, B - 2 + b)
                wait(pe, s_qc, b - 1)
                pe.matmul(ln_ps[b % 2][:, :], wq[:, :], g.XT[:, b * S:(b + 1) * S], start=True,
                          stop=True).then_inc(s_q, 1)
            pe.wait_ge(s_vd, 4)
            pe.wait_ge(s_kd, B)
            pe.wait_ge(s_qc, B)
            pe.wait_ge(w_in[3], 16)
            for step in range(NT + 6):
                n = step
                if n < NT:
                    wait(pe, s_l1, n - 1)
                    b, t = n // SB, n % SB
                    pe.matmul(logits[n % 2][:, :, :].rearrange("p h k -> p (h k)"), qt[:, b, t * P:(t + 1) * P],
                              kd[:, b, :], start=True, stop=True).then_inc(s_lg, 1)
                n = step - 2
                if 0 <= n < NT:
                    pe.wait_ge(s_w, n + 1)
                    wait(pe, s_wtc, n - 1)
                    for a in range(TURNS):
                        last = pe.transpose(turn[n % 2][:, a, :],
                                            w[n % 3][:, 4 * a:4 * a + 4, :].rearrange("p h k -> p (h k)"),
                                            g.ident[:, :])
                    last.then_inc(s_wt, 1)
                n = step - 3
                if 0 <= n < NT:
                    b, t = n // SB, n % SB
                    pe.wait_ge(s_wtc, n + 1)
                    wait(pe, s_on, n - 1)
                    for a in range(TURNS):
                        last = pe.matmul(o_ps[n % 2][:, 0, :], wt[n % 2][:, a, :], vd[:, b, a * P:(a + 1) * P],
                                         start=(a == 0), stop=(a == TURNS - 1))
                    last.then_inc(s_o, 1)
                n = step - 4
                if 0 <= n < NT:
                    b, t = n // SB, n % SB
                    pe.wait_ge(s_on, n + 1)
                    if t == 0:
                        wait(pe, s_otc, b - 1)
                        wait(pe, s_x, b - 1)
                    pe.transpose(ln_ps[b % 2][:, t * P:(t + 1) * P], on[n % 2][:, :], g.ident[:, :]).then_inc(s_ot, 1)
                n = step - 5
                if 0 <= n < NT and n % SB == SB - 1:
                    b = n // SB
                    pe.wait_ge(s_otc, b + 1)
                    for i in range(SB):
                        last = pe.matmul(ln_ps[b % 2][:, i * P:(i + 1) * P], ot[b % 2][:, i * P:(i + 1) * P],
                                         wo[:, :], start=True, stop=True)
                    last.then_inc(s_y, 1)

        @block.scalar
        def _(act):
            act.wait_ge(b_in, 64)
            act.wait_ge(s_kt, 1)
            act.activation(kt[:, :], logits[0][:, 0:4, :].rearrange("p a k -> p (a k)"), ACT.Identity,
                           bias=bqk[:, 1:2]).then_inc(s_ktc, 1)
            ln.scalar(act)
            for b in range(B):
                act.wait_ge(s_q, b + 1)
                act.activation(qt[:, b, :], ln_ps[b % 2][:, :], ACT.Identity, bias=bqk[:, 0:1]).then_inc(s_qc, 1)
            for step in range(NT + 6):
                n = step
                if n < NT:
                    act.wait_ge(s_z, n + 1)
                    act.activation(w[n % 3][:, :, :], w[n % 3][:, :, :], ACT.Exp).then_inc(s_e, 1)
                n = step - 2
                if 0 <= n < NT:
                    act.wait_ge(s_wt, n + 1)
                    wait(act, s_o, n - 1)
                    act.activation(wt[n % 2][:, :, :], turn[n % 2][:, :, :], ACT.Copy).then_inc(s_wtc, 1)
                n = step - 4
                if 0 <= n < NT and n % SB == SB - 1:
                    b = n // SB
                    act.wait_ge(s_ot, n + 1)
                    wait(act, s_y, b - 1)
                    act.activation(ot[b % 2][:, :], ln_ps[b % 2][:, :], ACT.Copy).then_inc(s_otc, 1)

        @block.vector
        def _(dve):
            ln.vector_stats(dve)
            dve.tensor_copy(ctx4[:, :, :, :], spread(g.ctx_t[:, :].rearrange("p (b k) -> p b k", k=KEYS), 2, 4)
                            ).then_inc(c4, 1)
            ln.vector_norm(dve)
            dve.wait_ge(s_ktc, 1)
            dve.wait_ge(hm, 3)
            for b in range(B):
                dve.tensor_tensor(kd[:, b, :].rearrange("p (h k) -> p h k", k=KEYS),
                                  spread(kt[:, b * KEYS:(b + 1) * KEYS], 1, H2), spread(hmask[:, :], 2, KEYS),
                                  ALU.mult).then_inc(s_kd, 1)
            dve.wait_ge(s_v, 1)
            dve.wait_ge(vz, 1)
            dve.wait_ge(b_in, 64)
            for q in range(4):
                rows = slice(KEYS * q, KEYS * q + KEYS)
                for b in range(B):
                    dst = vd[rows, b, :].rearrange("p (a w) -> p a w", w=160)[:, :, q * HD2:(q + 1) * HD2]
                    src = o_ps[0][rows, b, :].rearrange("p (a w) -> p a w", w=KEYS)[:, :, q * HD2:(q + 1) * HD2]
                    add = bv[rows, :].rearrange("p (a w) -> p a w", w=KEYS)[:, :, q * HD2:(q + 1) * HD2]
                    last = dve.tensor_tensor(dst, src, add, ALU.add)
                last.then_inc(s_vd, 1)
            dve.wait_ge(ln.norm, NT)
            for b in range(B):
                x = g.X[:, SB * b:SB * b + SB, :]
                last = dve.tensor_tensor(x, x, spread(bo[:, :], 1, SB), ALU.add)
            last.then_inc(s_xb, 1)
            dve.wait_ge(s_bias, 1)
            for step in range(NT + 6):
                n = step
                k = n % 3
                if n < NT:
                    dve.wait_ge(s_lg, n + 1)
                    wait(dve, s_wt, n - 2)
                    dve.scalar_tensor_tensor(out=w[k][:, :, :], in0=logits[n % 2][:, :, :],
                                             scalar=float(HD2) ** -0.5, in1=spread(bias[:, n, :], 1, H2),
                                             op0=ALU.mult, op1=ALU.add).then_inc(s_l1, 1)
                    dve.wait_ge(s_l1, n + 1)
                    dve.tensor_reduce(nmax[:, k, :], w[k][:, :, :], AX_X, ALU.max, negate=True).then_inc(s_nm, 1)
                    dve.wait_ge(s_nm, n + 1)
                    dve.tensor_tensor(w[k][:, :, :], w[k][:, :, :], spread(nmax[:, k, :], 2, KEYS),
                                      ALU.add).then_inc(s_z, 1)
                n = step - 1
                k = n % 3
                if 0 <= n < NT:
                    dve.wait_ge(s_e, n + 1)
                    wait(dve, s_on, n - 2)
                    dve.reduce_sum(rsum[:, k, :], w[k][:, :, :], AX_X).then_inc(s_sum, 1)
                    dve.wait_ge(s_sum, n + 1)
                    dve.reciprocal(rsum[:, k, :], rsum[:, k, :]).then_inc(s_r, 1)
                n = step - 3
                k = n % 3
                if 0 <= n < NT:
                    dve.wait_ge(s_o, n + 1)
                    dve.wait_ge(s_r, n + 1)
                    wait(dve, s_ot, n - 1)
                    dve.tensor_tensor(on[n % 2][:, :].rearrange("p (h d) -> p h d", d=HD2),
                                      o_ps[n % 2][:, 0, :].rearrange("p (h d) -> p h d", d=HD2),
                                      spread(rsum[:, k, :], 2, HD2), ALU.mult).then_inc(s_on, 1)
                n = step - 5
                if 0 <= n < NT and n % SB == SB - 1:
                    b = n // SB
                    dve.wait_ge(s_y, b + 1)
                    dve.wait_ge(s_xb, 1)
                    x = g.X[:, SB * b:SB * b + SB, :]
                    dve.tensor_tensor(x, x, ln_ps[b % 2][:, :].rearrange("p (t d) -> p t d", d=D),
                                      ALU.add).then_inc(s_x, 1)



FH = 512
FC = FH // P
GD = 16


def stage_mixture1(nc, g):
    with ExitStack() as ctx:
        sc = Scope(nc, ctx, "m1")
        ln_ps = [sc.ps(f"ln{i}", [P, 512]) for i in range(2)]
        ln = LayerNorm(sc, g, ln_ps)
        rt = Router(sc, g)
        up = [sc.ps(f"up{i}", [P, S]) for i in range(4)]
        down = [sc.ps(f"down{i}", [P, SB, D]) for i in range(2)]
        wgr = sc.sb("wgr", [GD, D])
        wgrt = sc.sb("wgrt", [P, GD])
        wg = sc.sb("wg", [E, GD])
        wsq = sc.sb("wsq", [E, GD])
        wnorm = sc.sb("wnorm", [E, 4])
        wgu = sc.sb("wgu", [E, GD])
        wgut = sc.sb("wgut", [GD, E])
        xr = sc.sb("xr", [GD, B * S])
        b1r = sc.sb("b1r", [E * FC, P])
        b1t = sc.sb("b1t", [P, E, FC])
        b1e = [sc.sb(f"b1e{i}", [P, FC]) for i in range(2)]
        b2r = sc.sb("b2r", [P, D])
        hmask = sc.sb("hmask", [P, NT])
        b2d = sc.sb("b2d", [P, NT, D])
        rtt = sc.sb("rtt", [P, P])
        rts = sc.sb("rts", [P, NT, E])
        w1 = [sc.sb(f"w1{i}", [P, FH]) for i in range(2)]
        w2 = [sc.sb(f"w2{i}", [P, FC, D]) for i in range(2)]
        hid = [sc.sb(f"hid{i}", [P, S]) for i in range(4)]
        w_in = [sc.sem(f"w_in{i}") for i in range(2)]
        (in_s, hm, prep, wn, wnd, prep_c, s_xr, s_xrc, s_b2, s_rts, s_rtt, s_rttc, s_bo, s_bx, s_up, s_h, s_dn,
         s_x, s_b1) = (sc.sem(n) for n in (
            "in", "mask", "prepared", "norm_pool", "norm", "prep_copied", "reduced", "reduced_copied", "b2_placed",
            "route_token", "route_turned", "route_copied", "bias_out", "bias_added", "up", "hidden", "down",
            "residual", "expert_biases"))
        block = sc.block()
        T = E * B

        def run(eng, body):
            body(0, True)
            with eng.Fori(1, E // 2) as r:
                body(r, False)

        @block.sync
        def _(sp):
            sp.dma_start(wgr[:, :], g.dram["L1_ffn_wg_red"]).then_inc(in_s, 16)
            sp.dma_start(wg[:, :], g.dram["L1_ffn_wg"]).then_inc(in_s, 16)
            sp.dma_start(b1r[:, :], g.dram["L1_ffn_b1"].rearrange("e (f p) -> (e f) p", p=P)).then_inc(in_s, 16)
            for n in range(NT):
                sp.dma_start(b2r[n * E:(n + 1) * E, :], g.dram["L1_ffn_b2"]).then_inc(in_s, 16)

            def body(r, first):
                for u in range(2):
                    e = 2 * r + u
                    if not first:
                        sp.wait_ge(s_dn, 4 * (e - 1))
                    sp.dma_start(w1[u][:, :], g.dram["L1_ffn_w1"][e]).then_inc(w_in[u], 16)
                    sp.dma_start(w2[u][:, :, :], g.dram["L1_ffn_w2"].rearrange("e (f p) d -> e p f d", p=P)[e]
                                 ).then_inc(w_in[u], 16)

            run(sp, body)

        @block.gpsimd
        def _(pool):
            pool.memset(hmask[:, :], 1.0).then_inc(hm, 1)
            pool.wait_ge(hm, 1)
            pool.affine_select(out=hmask[:, :], in_=hmask[:, :], compare_op=ALU.is_ge, fill=0.0, base=0,
                               pattern=[[-E, NT]], channel_multiplier=1).then_inc(hm, 1)
            pool.wait_ge(hm, 2)
            pool.affine_select(out=hmask[:, :], in_=hmask[:, :], compare_op=ALU.is_ge, fill=0.0, base=E - 1,
                               pattern=[[E, NT]], channel_multiplier=-1).then_inc(hm, 1)
            pool.wait_ge(wnd, 2)
            pool.tensor_tensor(wnorm[:, 2:3], wnorm[:, 0:1], wnorm[:, 1:2], ALU.pow).then_inc(wn, 1)
            ln.gpsimd(pool)

        @block.tensor
        def _(pe):
            pe.wait_ge(in_s, 16 * (3 + NT))
            pe.transpose(up[0][:, 0:GD], wgr[:, :], g.ident[0:GD, 0:GD]).then_inc(prep, 1)
            pe.transpose(up[1][:, 0:E * FC], b1r[:, :], g.ident[0:E * FC, 0:E * FC]).then_inc(prep, 1)
            pe.wait_ge(wnd, 5)
            pe.transpose(up[2][0:GD, 0:E], wgu[:, :], g.ident[0:E, 0:E]).then_inc(prep, 1)
            ln.tensor(pe)
            pe.wait_ge(prep_c, 3)
            for b in range(B):
                ln.ready(pe, b)
                pe.matmul(up[b][0:GD, :], wgrt[:, :], g.XT[:, b * S:(b + 1) * S], start=True, stop=True
                          ).then_inc(s_xr, 1)
            pe.wait_ge(s_xrc, B)
            for n in range(NT):
                last = pe.matmul(ln_ps[0][:, n * E:(n + 1) * E], xr[:, n * P:(n + 1) * P], wgut[:, :],
                                 start=True, stop=True)
            last.then_inc(rt.logit_s, 1)

            def down_part(v, f, k, first, last_):
                pe.wait_ge(s_h, v + 1)
                for i in range(SB):
                    mm = pe.matmul(down[k % 2][:, i, :], hid[f][:, i * P:(i + 1) * P], w2[(k // B) % 2][:, f, :],
                                   start=(f == 0 and i == 0), stop=(f == FC - 1), skip_group_check=True)
                if f == FC - 1:
                    mm.then_inc(s_dn, 1)

            def body(r, first):
                for u in range(2 * B):
                    t = 2 * B * r + u
                    if u % B == 0:
                        pe.wait_ge(w_in[u // B], 32 * (r + 1))
                    for f in range(FC):
                        v = FC * t + f
                        wait(pe, s_h, v - 3)
                        pe.matmul(up[f][:, :], w1[u // B][:, f * P:(f + 1) * P],
                                  g.XT[:, (u % B) * S:(u % B + 1) * S], start=True, stop=True).then_inc(s_up, 1)
                        if f >= 2:
                            if f == 2:
                                wait(pe, s_x, t - 1)
                            down_part(v - 2, f - 2, u, first, False)
                        elif not (first and u == 0):
                            down_part(v - 2, f + 2, (u - 1) % (2 * B), first, False)

            run(pe, body)
            for f in (2, 3):
                down_part(FC * T - 4 + f, f, 2 * B - 1, False, True)
            pe.wait_ge(s_rts, 1)
            pe.transpose(ln_ps[1][:, 0:P], rts[:, :, :].rearrange("p n e -> p (n e)"), g.ident[:, :]
                         ).then_inc(s_rtt, 1)
            pe.wait_ge(s_rttc, 1)
            pe.wait_ge(s_b2, 1)
            for b in range(B):
                pe.matmul(up[b][:, :], rtt[:, :], b2d[:, SB * b:SB * b + SB, :].rearrange("p n d -> p (n d)"),
                          start=True, stop=True).then_inc(s_bo, 1)

        @block.scalar
        def _(act):
            for i, (dst, src) in enumerate(((wgrt[:, :], up[0][:, 0:GD]), (b1t[:, :, :].rearrange("p e f -> p (e f)"), up[1][:, 0:E * FC]),
                                            (wgut[:, :], up[2][0:GD, 0:E]))):
                act.wait_ge(prep, i + 1)
                act.activation(dst, src, ACT.Copy).then_inc(prep_c, 1)
            ln.scalar(act)
            for b in range(B):
                act.wait_ge(s_xr, b + 1)
                act.activation(xr[:, b * S:(b + 1) * S], up[b][0:GD, :], ACT.Copy).then_inc(s_xrc, 1)
            rt.scalar(act)

            def body(r, first):
                for u in range(2 * B):
                    t = 2 * B * r + u
                    if u % B == 0:
                        act.wait_ge(s_b1, 2 * r + u // B + 1)
                    for f in range(FC):
                        v = FC * t + f
                        act.wait_ge(s_up, v + 1)
                        if f >= 2:
                            wait(act, s_dn, t)
                        elif f == 0:
                            wait(act, s_dn, t - 1)
                        act.activation(hid[f][:, :], up[f][:, :], ACT.Gelu, bias=b1e[u // B][:, f:f + 1]
                                       ).then_inc(s_h, 1)

            run(act, body)
            act.wait_ge(s_rtt, 1)
            act.activation(rtt[:, :], ln_ps[1][:, 0:P], ACT.Copy).then_inc(s_rttc, 1)

        @block.vector
        def _(dve):
            dve.memset(wnorm[:, 1:2], 0.5).then_inc(wnd, 1)
            dve.wait_ge(in_s, 16 * (3 + NT))
            dve.tensor_tensor_reduce(out=wsq[:, :], in0=wg[:, :], in1=wg[:, :], scale=1.0, scalar=0.0,
                                     op0=ALU.mult, op1=ALU.add, accum_out=wnorm[:, 0:1]).then_inc(wnd, 1)
            dve.wait_ge(wn, 1)
            dve.tensor_scalar(wnorm[:, 2:3], wnorm[:, 2:3], 1e-4, None, ALU.max).then_inc(wnd, 1)
            dve.wait_ge(wnd, 3)
            dve.reciprocal(wnorm[:, 3:4], wnorm[:, 2:3]).then_inc(wnd, 1)
            dve.wait_ge(wnd, 4)
            dve.tensor_scalar(wgu[:, :], wg[:, :], wnorm[:, 3:4], None, ALU.mult).then_inc(wnd, 1)
            ln.vector_stats(dve)
            ln.vector_norm(dve)
            rt.top1(dve, ln_ps[0][:, 0:NT * E].rearrange("p (n e) -> p n e", e=E))
            dve.wait_ge(rt.done, 1)
            dve.tensor_copy(rts[:, :, :], rt.route[:, :, :].rearrange("p e n -> p n e")).then_inc(s_rts, 1)
            dve.wait_ge(hm, 3)
            dve.tensor_tensor(b2d[:, :, :], spread(b2r[:, :], 1, NT), spread(hmask[:, :], 2, D),
                              ALU.mult).then_inc(s_b2, 1)

            def body(r, first):
                for u in range(2 * B):
                    t = 2 * B * r + u
                    e = 2 * r + u // B
                    dve.wait_ge(s_dn, t + 1)
                    for i in range(SB):
                        n = SB * (u % B) + i
                        x = g.X[:, n, :]
                        last = dve.scalar_tensor_tensor(out=x, in0=down[u % 2][:, i, :],
                                                        scalar=rt.route[:, e, n:n + 1], in1=x, op0=ALU.mult,
                                                        op1=ALU.add)
                    last.then_inc(s_x, 1)
                    if u % B == 0:
                        dve.tensor_copy(b1e[1 - u // B][:, :], b1t[:, (e + 1) % E, :]).then_inc(s_b1, 1)

            dve.wait_ge(prep_c, 3)
            dve.tensor_copy(b1e[0][:, :], b1t[:, 0, :]).then_inc(s_b1, 1)
            run(dve, body)
            dve.wait_ge(s_x, T)
            for b in range(B):
                dve.wait_ge(s_bo, b + 1)
                x = g.X[:, SB * b:SB * b + SB, :]
                dve.tensor_tensor(x, x, up[b][:, :].rearrange("p (n d) -> p n d", d=D), ALU.add).then_inc(s_bx, 1)


def stage_store(nc, g, out):
    with ExitStack() as ctx:
        sc = Scope(nc, ctx, "st")
        stored = sc.sem("stored")
        block = sc.block()

        @block.sync
        def _(sp):
            for b in range(B):
                sp.dma_start(out[b].rearrange("(t p) d -> p t d", p=P), g.X[:, SB * b:SB * b + SB, :]).then_inc(stored, 16)
            sp.wait_ge(stored, 16 * B)


def decoder(nc, dram, out, stages=6):
    with ExitStack() as ctx:
        sc = Scope(nc, ctx, "g")
        g = Globals()
        g.dram = dram
        g.X = sc.sb("X", [P, NT, D])
        g.XN = sc.sb("XN", [P, NT, D])
        g.XT = sc.sb("XT", [P, B * S])
        g.ident = sc.sb("ident", [P, P])
        g.ident16 = sc.sb("ident16", [P, P], BF16)
        g.mhalf = sc.sb("mhalf", [P, 64])
        g.wo0 = sc.sb("wo0", [P, D])
        g.rank = sc.sb("rank", [P, E])
        g.ctx_t = sc.sb("ctx_t", [P, B * KEYS])
        g.weights = {"wo0": (g.wo0[:, :], dram["L0_attn_wo"])}
        g.w_in = {name: sc.sem("in_" + name) for name in g.weights}
        with ExitStack() as ctx0:
            s0 = Scope(nc, ctx0, "t")
            g.a_unit = s0.sb("a_unit", [P, UNITS, SB, 2, HD0])
            g.v_tok = s0.sb("v_tok", [P, UNITS, SB, 2 * HD0])
            with ExitStack() as ctx1:
                s1 = Scope(nc, ctx1, "u")
                g.q_tok = s1.sb("q_tok", [P, UNITS, SB, 4 * W0], BF16)
                g.k_tok = s1.sb("k_tok", [P, UNITS, SB, 4 * W0], BF16)
                stage_project0(nc, g, dram, out)
                stage_attention0(nc, g)
            stage_output0(nc, g)
        for stage in (stage_cross0, stage_mixture0, stage_attention1, stage_cross1, stage_mixture1)[:stages - 1]:
            stage(nc, g)
        stage_store(nc, g, out)


def kernel(**inputs):
    import numpy as _np
    import concourse.bacc as _bacc
    from concourse.bass_utils import run_bass_kernel_spmd as _run

    nc = _bacc.Bacc("TRN2", target_bir_lowering=False, num_devices=1)
    arrays, dram = {}, {}
    for name in INPUTS:
        a = _np.ascontiguousarray(inputs[name])
        arrays[name] = a
        dram[name] = nc.dram_tensor(name, a.shape, mybir.dt.from_np(a.dtype), kind="ExternalInput").ap()
    out = nc.dram_tensor("out", (B, S, D), F32, kind="ExternalOutput").ap()
    decoder(nc, dram, out)
    r = _run(nc, [arrays], core_ids=[0])
    return r.results[0]["out"]
```
